# Optimizing a Trainium2 kernel written in Bass

```python
import numpy as np
import jax
import jax.numpy as jnp

def _softmax(x, axis=-1):
    return jax.nn.softmax(x, axis=axis)

def _gelu(x):
    return jax.nn.gelu(x, approximate=True)

def _silu(x):
    return jax.nn.silu(x)

def _sigmoid(x):
    return jax.nn.sigmoid(x)

def _layernorm(x, axis=-1, eps=1e-05):
    m = jnp.mean(x, axis=axis, keepdims=True)
    v = jnp.var(x, axis=axis, keepdims=True)
    return (x - m) / jnp.sqrt(v + eps)

def _scatter_add(tgt, idx, src, axis=0):
    return tgt.at[idx].add(src)

def _segment_sum(src, seg, n):
    return jax.ops.segment_sum(src, seg, n)
kernel_name = 'mk_conv_seq_d2_conv_nhwc256_r2_77eefb'

def setup_inputs(seed: int=0):
    np.random.seed(seed)
    _w = jnp.asarray

    def _rec_inputs():
        import jax
        import jax.numpy as jnp
        _gk = jax.random.key(seed)
        x = -0.000125 + 0.9999 * jax.random.normal(jax.random.fold_in(_gk, 1), (2, 128, 128, 128), jnp.float32)
        return x
    x = _rec_inputs()

    def _L0_conv_setup():
        import jax, jax.numpy as jnp
        import numpy as np
        EPS = 1e-05
        LAM = 0.01
        NUM_BLOCKS = 8

        def layer_norm(x, g, b):
            mu = jnp.mean(x, axis=-1, keepdims=True)
            var = jnp.mean(jnp.square(x - mu), axis=-1, keepdims=True)
            return (x - mu) * jax.lax.rsqrt(var + EPS) * g + b

        def softshrink(v, lam):
            return jnp.where(jnp.abs(v) > lam, v - jnp.sign(v) * lam, jnp.zeros_like(v))

        def afno_filter(x, w1, b1, w2, b2):
            B, H, W, C = x.shape
            bs = C // NUM_BLOCKS
            xf = jnp.fft.rfft2(x, axes=(1, 2), norm='ortho')
            xf = xf.reshape(B, H, W // 2 + 1, NUM_BLOCKS, bs)
            xr, xi = (jnp.real(xf), jnp.imag(xf))
            o1r = jax.nn.relu(jnp.einsum('bhwni,nio->bhwno', xr, w1[0]) - jnp.einsum('bhwni,nio->bhwno', xi, w1[1]) + b1[0])
            o1i = jax.nn.relu(jnp.einsum('bhwni,nio->bhwno', xi, w1[0]) + jnp.einsum('bhwni,nio->bhwno', xr, w1[1]) + b1[1])
            o2r = jnp.einsum('bhwni,nio->bhwno', o1r, w2[0]) - jnp.einsum('bhwni,nio->bhwno', o1i, w2[1]) + b2[0]
            o2i = jnp.einsum('bhwni,nio->bhwno', o1i, w2[0]) + jnp.einsum('bhwni,nio->bhwno', o1r, w2[1]) + b2[1]
            o2r = softshrink(o2r, LAM)
            o2i = softshrink(o2i, LAM)
            yf = (o2r + 1j * o2i).reshape(B, H, W // 2 + 1, C)
            y = jnp.fft.irfft2(yf, s=(H, W), axes=(1, 2), norm='ortho')
            return y + x
        key = jax.random.key(seed)
        ks = jax.random.split(key, 16)
        B, H, W, C = (2, 128, 128, 128)
        bs = C // NUM_BLOCKS
        latent = 4 * C
        scale = 0.02
        return {'x': jax.random.normal(ks[0], (B, H, W, C), dtype=jnp.float32), 'n1_g': jnp.ones((C,), jnp.float32), 'n1_b': jnp.zeros((C,), jnp.float32), 'n2_g': jnp.ones((C,), jnp.float32), 'n2_b': jnp.zeros((C,), jnp.float32), 'w1': scale * jax.random.normal(ks[1], (2, NUM_BLOCKS, bs, bs), jnp.float32), 'b1': scale * jax.random.normal(ks[2], (2, NUM_BLOCKS, bs), jnp.float32), 'w2': scale * jax.random.normal(ks[3], (2, NUM_BLOCKS, bs, bs), jnp.float32), 'b2': scale * jax.random.normal(ks[4], (2, NUM_BLOCKS, bs), jnp.float32), 'mw1': jax.random.normal(ks[5], (C, latent), jnp.float32) / np.sqrt(C), 'mb1': jnp.zeros((latent,), jnp.float32), 'mw2': jax.random.normal(ks[6], (latent, C), jnp.float32) / np.sqrt(latent), 'mb2': jnp.zeros((C,), jnp.float32)}
    _L0_conv_all = _L0_conv_setup()
    _L0_conv_in = {k: v for k, v in _L0_conv_all.items() if k in ('n1_g', 'n1_b', 'n2_g', 'n2_b', 'w1', 'b1', 'w2', 'b2', 'mw1', 'mb1', 'mw2', 'mb2')}
    del _L0_conv_all

    def _L1_conv_setup():
        import jax, jax.numpy as jnp
        import numpy as np
        EPS = 1e-05
        LAM = 0.01
        NUM_BLOCKS = 8

        def layer_norm(x, g, b):
            mu = jnp.mean(x, axis=-1, keepdims=True)
            var = jnp.mean(jnp.square(x - mu), axis=-1, keepdims=True)
            return (x - mu) * jax.lax.rsqrt(var + EPS) * g + b

        def softshrink(v, lam):
            return jnp.where(jnp.abs(v) > lam, v - jnp.sign(v) * lam, jnp.zeros_like(v))

        def afno_filter(x, w1, b1, w2, b2):
            B, H, W, C = x.shape
            bs = C // NUM_BLOCKS
            xf = jnp.fft.rfft2(x, axes=(1, 2), norm='ortho')
            xf = xf.reshape(B, H, W // 2 + 1, NUM_BLOCKS, bs)
            xr, xi = (jnp.real(xf), jnp.imag(xf))
            o1r = jax.nn.relu(jnp.einsum('bhwni,nio->bhwno', xr, w1[0]) - jnp.einsum('bhwni,nio->bhwno', xi, w1[1]) + b1[0])
            o1i = jax.nn.relu(jnp.einsum('bhwni,nio->bhwno', xi, w1[0]) + jnp.einsum('bhwni,nio->bhwno', xr, w1[1]) + b1[1])
            o2r = jnp.einsum('bhwni,nio->bhwno', o1r, w2[0]) - jnp.einsum('bhwni,nio->bhwno', o1i, w2[1]) + b2[0]
            o2i = jnp.einsum('bhwni,nio->bhwno', o1i, w2[0]) + jnp.einsum('bhwni,nio->bhwno', o1r, w2[1]) + b2[1]
            o2r = softshrink(o2r, LAM)
            o2i = softshrink(o2i, LAM)
            yf = (o2r + 1j * o2i).reshape(B, H, W // 2 + 1, C)
            y = jnp.fft.irfft2(yf, s=(H, W), axes=(1, 2), norm='ortho')
            return y + x
        key = jax.random.key(seed)
        ks = jax.random.split(key, 16)
        B, H, W, C = (2, 128, 128, 128)
        bs = C // NUM_BLOCKS
        latent = 4 * C
        scale = 0.02
        return {'x': jax.random.normal(ks[0], (B, H, W, C), dtype=jnp.float32), 'n1_g': jnp.ones((C,), jnp.float32), 'n1_b': jnp.zeros((C,), jnp.float32), 'n2_g': jnp.ones((C,), jnp.float32), 'n2_b': jnp.zeros((C,), jnp.float32), 'w1': scale * jax.random.normal(ks[1], (2, NUM_BLOCKS, bs, bs), jnp.float32), 'b1': scale * jax.random.normal(ks[2], (2, NUM_BLOCKS, bs), jnp.float32), 'w2': scale * jax.random.normal(ks[3], (2, NUM_BLOCKS, bs, bs), jnp.float32), 'b2': scale * jax.random.normal(ks[4], (2, NUM_BLOCKS, bs), jnp.float32), 'mw1': jax.random.normal(ks[5], (C, latent), jnp.float32) / np.sqrt(C), 'mb1': jnp.zeros((latent,), jnp.float32), 'mw2': jax.random.normal(ks[6], (latent, C), jnp.float32) / np.sqrt(latent), 'mb2': jnp.zeros((C,), jnp.float32)}
    _L1_conv_all = _L1_conv_setup()
    _L1_conv_in = {k: v for k, v in _L1_conv_all.items() if k in ('n1_g', 'n1_b', 'n2_g', 'n2_b', 'w1', 'b1', 'w2', 'b2', 'mw1', 'mb1', 'mw2', 'mb2')}
    del _L1_conv_all
    return {'x': x, 'L0_conv_n1_g': _L0_conv_in['n1_g'], 'L0_conv_n1_b': _L0_conv_in['n1_b'], 'L0_conv_n2_g': _L0_conv_in['n2_g'], 'L0_conv_n2_b': _L0_conv_in['n2_b'], 'L0_conv_w1': _L0_conv_in['w1'], 'L0_conv_b1': _L0_conv_in['b1'], 'L0_conv_w2': _L0_conv_in['w2'], 'L0_conv_b2': _L0_conv_in['b2'], 'L0_conv_mw1': _L0_conv_in['mw1'], 'L0_conv_mb1': _L0_conv_in['mb1'], 'L0_conv_mw2': _L0_conv_in['mw2'], 'L0_conv_mb2': _L0_conv_in['mb2'], 'L1_conv_n1_g': _L1_conv_in['n1_g'], 'L1_conv_n1_b': _L1_conv_in['n1_b'], 'L1_conv_n2_g': _L1_conv_in['n2_g'], 'L1_conv_n2_b': _L1_conv_in['n2_b'], 'L1_conv_w1': _L1_conv_in['w1'], 'L1_conv_b1': _L1_conv_in['b1'], 'L1_conv_w2': _L1_conv_in['w2'], 'L1_conv_b2': _L1_conv_in['b2'], 'L1_conv_mw1': _L1_conv_in['mw1'], 'L1_conv_mb1': _L1_conv_in['mb1'], 'L1_conv_mw2': _L1_conv_in['mw2'], 'L1_conv_mb2': _L1_conv_in['mb2']}

def reference(x, L0_conv_n1_g, L0_conv_n1_b, L0_conv_n2_g, L0_conv_n2_b, L0_conv_w1, L0_conv_b1, L0_conv_w2, L0_conv_b2, L0_conv_mw1, L0_conv_mb1, L0_conv_mw2, L0_conv_mb2, L1_conv_n1_g, L1_conv_n1_b, L1_conv_n2_g, L1_conv_n2_b, L1_conv_w1, L1_conv_b1, L1_conv_w2, L1_conv_b2, L1_conv_mw1, L1_conv_mb1, L1_conv_mw2, L1_conv_mb2):
    import jax
    import jax.numpy as jnp

    def _L0_conv_ref(x, n1_g, n1_b, n2_g, n2_b, w1, b1, w2, b2, mw1, mb1, mw2, mb2):
        import jax, jax.numpy as jnp
        import numpy as np
        EPS = 1e-05
        LAM = 0.01
        NUM_BLOCKS = 8

        def layer_norm(x, g, b):
            mu = jnp.mean(x, axis=-1, keepdims=True)
            var = jnp.mean(jnp.square(x - mu), axis=-1, keepdims=True)
            return (x - mu) * jax.lax.rsqrt(var + EPS) * g + b

        def softshrink(v, lam):
            return jnp.where(jnp.abs(v) > lam, v - jnp.sign(v) * lam, jnp.zeros_like(v))

        def afno_filter(x, w1, b1, w2, b2):
            B, H, W, C = x.shape
            bs = C // NUM_BLOCKS
            xf = jnp.fft.rfft2(x, axes=(1, 2), norm='ortho')
            xf = xf.reshape(B, H, W // 2 + 1, NUM_BLOCKS, bs)
            xr, xi = (jnp.real(xf), jnp.imag(xf))
            o1r = jax.nn.relu(jnp.einsum('bhwni,nio->bhwno', xr, w1[0]) - jnp.einsum('bhwni,nio->bhwno', xi, w1[1]) + b1[0])
            o1i = jax.nn.relu(jnp.einsum('bhwni,nio->bhwno', xi, w1[0]) + jnp.einsum('bhwni,nio->bhwno', xr, w1[1]) + b1[1])
            o2r = jnp.einsum('bhwni,nio->bhwno', o1r, w2[0]) - jnp.einsum('bhwni,nio->bhwno', o1i, w2[1]) + b2[0]
            o2i = jnp.einsum('bhwni,nio->bhwno', o1i, w2[0]) + jnp.einsum('bhwni,nio->bhwno', o1r, w2[1]) + b2[1]
            o2r = softshrink(o2r, LAM)
            o2i = softshrink(o2i, LAM)
            yf = (o2r + 1j * o2i).reshape(B, H, W // 2 + 1, C)
            y = jnp.fft.irfft2(yf, s=(H, W), axes=(1, 2), norm='ortho')
            return y + x
        residual = x
        h = layer_norm(x, n1_g, n1_b)
        h = afno_filter(h, w1, b1, w2, b2)
        h = h + residual
        residual = h
        h = layer_norm(h, n2_g, n2_b)
        h = jax.nn.gelu(h @ mw1 + mb1, approximate=False)
        h = h @ mw2 + mb2
        return h + residual

    def _L1_conv_ref(x, n1_g, n1_b, n2_g, n2_b, w1, b1, w2, b2, mw1, mb1, mw2, mb2):
        import jax, jax.numpy as jnp
        import numpy as np
        EPS = 1e-05
        LAM = 0.01
        NUM_BLOCKS = 8

        def layer_norm(x, g, b):
            mu = jnp.mean(x, axis=-1, keepdims=True)
            var = jnp.mean(jnp.square(x - mu), axis=-1, keepdims=True)
            return (x - mu) * jax.lax.rsqrt(var + EPS) * g + b

        def softshrink(v, lam):
            return jnp.where(jnp.abs(v) > lam, v - jnp.sign(v) * lam, jnp.zeros_like(v))

        def afno_filter(x, w1, b1, w2, b2):
            B, H, W, C = x.shape
            bs = C // NUM_BLOCKS
            xf = jnp.fft.rfft2(x, axes=(1, 2), norm='ortho')
            xf = xf.reshape(B, H, W // 2 + 1, NUM_BLOCKS, bs)
            xr, xi = (jnp.real(xf), jnp.imag(xf))
            o1r = jax.nn.relu(jnp.einsum('bhwni,nio->bhwno', xr, w1[0]) - jnp.einsum('bhwni,nio->bhwno', xi, w1[1]) + b1[0])
            o1i = jax.nn.relu(jnp.einsum('bhwni,nio->bhwno', xi, w1[0]) + jnp.einsum('bhwni,nio->bhwno', xr, w1[1]) + b1[1])
            o2r = jnp.einsum('bhwni,nio->bhwno', o1r, w2[0]) - jnp.einsum('bhwni,nio->bhwno', o1i, w2[1]) + b2[0]
            o2i = jnp.einsum('bhwni,nio->bhwno', o1i, w2[0]) + jnp.einsum('bhwni,nio->bhwno', o1r, w2[1]) + b2[1]
            o2r = softshrink(o2r, LAM)
            o2i = softshrink(o2i, LAM)
            yf = (o2r + 1j * o2i).reshape(B, H, W // 2 + 1, C)
            y = jnp.fft.irfft2(yf, s=(H, W), axes=(1, 2), norm='ortho')
            return y + x
        residual = x
        h = layer_norm(x, n1_g, n1_b)
        h = afno_filter(h, w1, b1, w2, b2)
        h = h + residual
        residual = h
        h = layer_norm(h, n2_g, n2_b)
        h = jax.nn.gelu(h @ mw1 + mb1, approximate=False)
        h = h @ mw2 + mb2
        return h + residual

    def _gn(v, G=32, eps=1e-05):
        B_, H_, W_, C_ = v.shape
        g = v.reshape(B_, H_, W_, G, C_ // G)
        m = jnp.mean(g, axis=(1, 2, 4), keepdims=True)
        s = jnp.var(g, axis=(1, 2, 4), keepdims=True)
        return ((g - m) / jnp.sqrt(s + eps)).reshape(v.shape)

    def _ln_c(v, eps=1e-06):
        m = jnp.mean(v, axis=-1, keepdims=True)
        s = jnp.var(v, axis=-1, keepdims=True)
        return (v - m) / jnp.sqrt(s + eps)

    def _ln_t(v, eps=1e-05):
        m = jnp.mean(v, axis=-1, keepdims=True)
        s = jnp.var(v, axis=-1, keepdims=True)
        return (v - m) / jnp.sqrt(s + eps)

    def _to_tokens(v):
        B_, H_, W_, C_ = v.shape
        return v.reshape(B_, H_ * W_, C_)

    def _from_tokens(t, like):
        return t.reshape(like.shape)
    x = _L0_conv_ref(x, L0_conv_n1_g, L0_conv_n1_b, L0_conv_n2_g, L0_conv_n2_b, L0_conv_w1, L0_conv_b1, L0_conv_w2, L0_conv_b2, L0_conv_mw1, L0_conv_mb1, L0_conv_mw2, L0_conv_mb2)
    x = _L1_conv_ref(x, L1_conv_n1_g, L1_conv_n1_b, L1_conv_n2_g, L1_conv_n2_b, L1_conv_w1, L1_conv_b1, L1_conv_w2, L1_conv_b2, L1_conv_mw1, L1_conv_mb1, L1_conv_mw2, L1_conv_mb2)
    return x

_drawn_inputs = setup_inputs


def setup_inputs(seed=0):
    import zlib

    import numpy as np

    out = dict(_drawn_inputs(seed))
    spreads = {'L0_conv_n1_g': (1.0, 0.2),
     'L0_conv_n1_b': (0.0, 0.1),
     'L0_conv_n2_g': (1.0, 0.2),
     'L0_conv_n2_b': (0.0, 0.279),
     'L0_conv_mb1': (0.0, 0.267),
     'L0_conv_mb2': (0.0, 0.1),
     'L1_conv_n1_g': (1.0, 0.2),
     'L1_conv_n1_b': (0.0, 0.267),
     'L1_conv_n2_g': (1.0, 0.2),
     'L1_conv_n2_b': (0.0, 0.379),
     'L1_conv_mb1': (0.0, 0.381),
     'L1_conv_mb2': (0.0, 0.268)}
    factors = {'L0_conv_w1': 8.0,
     'L0_conv_b1': 8.0,
     'L0_conv_w2': 8.0,
     'L0_conv_b2': 6.823,
     'L1_conv_w1': 8.0,
     'L1_conv_b1': 8.0,
     'L1_conv_w2': 8.0,
     'L1_conv_b2': 8.0}
    for name, (base, spread) in spreads.items():
        noise = np.random.default_rng([zlib.crc32(name.encode()), seed]).standard_normal(out[name].shape)
        drawn = base * np.exp(spread * noise) if base else spread * noise
        out[name] = jnp.asarray(drawn.astype(out[name].dtype))
    for name, factor in factors.items():
        out[name] = (out[name] * factor).astype(out[name].dtype)
    return out
```

```python
from contextlib import ExitStack

import numpy as np

import concourse.bass as bass
from concourse import mybir

F32 = mybir.dt.float32
F32R = mybir.dt.float32r
I32 = mybir.dt.int32
ALU = mybir.AluOpType
ACT = mybir.ActivationFunctionType

P = 128
IMAGES, LAYERS = 2, 2
H = W = C = 128
HALF = C // 2
BLOCK = 16
BLOCKS = HALF // BLOCK
LATENT = 4 * C
CHUNKS = LATENT // P
KWS = W // 2
ROWS = 4
TILES = H // ROWS
TOK = ROWS * W
GROUP = 4
CGROUPS = C // GROUP
BATCHES = KWS // GROUP
UNITS = 2 * BATCHES + 2
LN_EPS = 1e-5
LAM = 0.01
DC = float(np.sqrt(H * W))
MAGIC = float(0x5F3759DF - 2 ** 22 - 2 ** 30)
STEPS = [(layer, image) for layer in range(LAYERS) for image in range(IMAGES)]
LAG = 3
PRO_ACT = 3
CONSTS = 6 * P + 4 * BLOCKS
PB = 8
Z_DVE0 = (PB - PRO_ACT) * (TILES // PB)
STATS = TILES + LAG
SPEC_IN = 16 * 4
MLP_IN = 16 * 4
X_CREDIT = 2


def dft_constants():
    n = np.arange(P, dtype=np.float64)
    turn = 2 * np.pi / P
    scale = 1 / np.sqrt(P)
    k = np.arange(KWS + 1, dtype=np.float64)
    cos = np.cos(turn * np.outer(n, k)) * scale
    sin = np.sin(turn * np.outer(n, k)) * scale
    fw = np.stack([cos[:, :KWS], -sin[:, :KWS]], 2)
    fw[:, 0, 1] = cos[:, KWS]
    cas = (np.cos(turn * np.outer(n, n)) + np.sin(turn * np.outer(n, n))) * scale
    d1 = np.stack([cos - sin, -cos - sin], 2)[:, :KWS]
    d2 = np.stack([cos + sin, cos - sin], 2)[:, :KWS]
    d1[:, 0, 0], d1[:, 0, 1] = cos[:, 0], cos[:, KWS]
    d2[:, 0] = 0
    reverse = np.zeros((P, P))
    reverse[np.arange(P), -np.arange(P) % P] = 1
    block = (np.arange(P) % HALF) // BLOCK
    mask = (block[:, None] == np.arange(BLOCKS)[None]).astype(np.float64)
    parts = [fw.reshape(P, P), cas, d1.reshape(P, P).T, d2.reshape(P, P).T, np.eye(P), reverse]
    return np.concatenate([*parts, mask, -mask, mask / 2, -mask / 2], 1).astype(np.float32)


class Chain:

    def __init__(self, eng, sem):
        self.eng, self.sem, self.base, self.trip, self.n = eng, sem, 0, None, 0

    def add(self, ins):
        ins.then_inc(self.sem, 1)
        self.n += 1

    def settle(self):
        at = self.base + self.n
        self.eng.wait_ge(self.sem, at if self.trip is None else self.trip * self.per + at)

    def enter(self, trip, per, first):
        self.base, self.n, self.trip, self.per = self.base + self.n - first * per, 0, trip, per

    def leave(self, end):
        assert self.n == self.per, self.n
        self.base, self.n, self.trip = self.base + end * self.per, 0, None


def afno(nc, x, consts, params, out):
    ctx = ExitStack()
    with ctx:
        top = [(nc.sbuf_base + 63) // 64 * 64]

        def at(name, shape, offset, dtype=F32):
            return nc.alloc_sbuf_tensor_at(name, shape, dtype, offset=offset)

        def size(shape):
            return int(np.prod(shape[1:])) * 4

        def sb(name, shape, dtype=F32):
            offset = top[0]
            top[0] = (offset + size(shape) + 31) // 32 * 32
            return at(name, shape, offset, dtype)

        def sem(name):
            return ctx.enter_context(nc.semaphore(name))

        resid = sb("resid", [P, H, C])
        zbuf_at = top[0]
        zbuf = sb("zbuf", [P, H + 1, C])
        spec_at = top[0]
        spec = sb("spec", [P, KWS, 2, HALF, 2])
        spec_end = top[0]
        cst = sb("cst", [P, CONSTS])
        FW, CAS, D1, D2, IDENT, REVERSE = (cst[:, i * P:(i + 1) * P] for i in range(6))
        mask = cst[:, 6 * P:].rearrange("p (s b) -> p s b", s=4)
        w1s = sb("w1s", [P, 3, 2, 2, HALF])
        w2s = sb("w2s", [P, 2, 2, HALF])
        wraw = sb("wraw", [P, 2, 2, 2, BLOCK])
        wsum = sb("wsum", [P, 2, 2, BLOCK])
        vectors = sb("vectors", [P, 4, 2])
        gain64, beta64, b1v, dcbias = (vectors[:, i, :] for i in range(4))
        b2rep = sb("b2rep", [P, 2, 2, HALF])
        betarow = sb("betarow", [P, C])
        gain1 = sb("gain1", [P, C])
        columns = sb("columns", [P, 2 + CHUNKS])
        gain2, beta2, mb1 = columns[:, 0:1], columns[:, 1:2], columns[:, 2:]
        mb1f = sb("mb1f", [P, CHUNKS])
        stats = sb("stats", [P, 4, 2 * ROWS, 3])
        rstd = sb("rstd", [P, 4, 2 * ROWS])
        var = sb("var", [P, 4, 2 * ROWS])
        nt0 = sb("nt0", [P, 2 * ROWS])
        c15 = sb("c15", [P, 2 * ROWS])
        xout = sb("xout", [P, 2, ROWS, C])
        assert top[0] <= nc.sbuf_usable_end, (top[0], nc.sbuf_usable_end)

        o = zbuf_at
        gsb = at("gsb", [P, 2, P, GROUP], o); o += size(gsb.shape)
        osb = at("osb", [P, 2, P, GROUP], o); o += size(osb.shape)
        vsb = at("vsb", [P, 2, GROUP, 2, HALF], o); o += size(vsb.shape)
        csb = at("csb", [P, 2, GROUP, 2, HALF], o); o += size(csb.shape)
        nyq = at("nyq", [P, 2, P], o); o += size(nyq.shape)
        yedge = at("yedge", [P, 2, 2, HALF, 2], o); o += size(yedge.shape)
        tedge = at("tedge", [P, 2, 2, C], o); o += size(tedge.shape)
        assert o <= spec_at
        o = spec_at
        xnext = at("xnext", [P, 4, ROWS, C], o); o += size(xnext.shape)
        gz = at("gz", [P, 2, ROWS, C], o); o += size(gz.shape)
        hn = at("hn", [P, 2, ROWS, C], o); o += size(hn.shape)
        hth = at("hth", [P, 2, TOK], o, F32R); o += size(hth.shape)
        htl = at("htl", [P, 2, TOK], o, F32R); o += size(htl.shape)
        gel = at("gel", [P, 2, CHUNKS, TOK], o); o += size(gel.shape)
        mw1raw = at("mw1raw", [P, LATENT], o); o += size(mw1raw.shape)
        mw1h = at("mw1h", [P, LATENT], o, F32R); o += size(mw1h.shape)
        mw1l = at("mw1l", [P, LATENT], o, F32R); o += size(mw1l.shape)
        mw2 = at("mw2", [P, CHUNKS, C], o); o += size(mw2.shape)
        mb2rep = at("mb2rep", [P, C], o); o += size(mb2rep.shape)
        assert o <= spec_end
        pst = at("pst", [P, TILES * ROWS, 3], o); o += size(pst.shape)
        prs = at("prs", [P, TILES * ROWS], o); o += size(prs.shape)
        pnm = at("pnm", [P, TILES * ROWS], o); o += size(pnm.shape)
        pva = at("pva", [P, PB * ROWS], o); o += size(pva.shape)
        pn0 = at("pn0", [P, PB * ROWS], o); o += size(pn0.shape)
        p15 = at("p15", [P, PB * ROWS], o); o += size(p15.shape)
        assert o <= spec_end

        ps = ctx.enter_context(nc.psum_tensor("ps", [P, 8, 512], F32))
        between = nc.dram_tensor("between", [IMAGES, H, W, C], F32).ap()

        cst_in = sem("cst_in")
        x_in = [sem(f"x_in{b}") for b in range(TILES // PB)]
        spec_in, gain_in, mlp_in = sem("spec_in"), sem("gain_in"), sem("mlp_in")
        spec_built, dc_mm, spec_done = sem("spec_built"), sem("dc_mm"), sem("spec_done")
        st_pro, z_dve, z_act, gz_done, r_done = (sem(n) for n in ("st_pro", "z_dve", "z_act", "gz_done", "r_done"))
        s1_mm, a_act, a_dve = (sem(n) for n in ("s1_mm", "a_act", "a_dve"))
        s2_mm, m1_mm, m2_mm = sem("s2_mm"), sem("m1_mm"), sem("m2_mm")
        g_out, o_out, v_out, y_done = sem("g_out"), sem("o_out"), sem("v_out"), sem("y_done")
        t_edge, x_mm = sem("t_edge"), sem("x_mm")
        ih_mm, v_act, v_dve, v_wrap = sem("ih_mm"), sem("v_act"), sem("v_dve"), sem("v_wrap")
        mlp_w, mlp_b_mm, mlp_b = sem("mlp_w"), sem("mlp_b_mm"), sem("mlp_b")
        iw_mm, h2_done, st_done, rs_done = sem("iw_mm"), sem("h2_done"), sem("st_done"), sem("rs_done")
        hn_done, t_mm, hi_out, lo_out = sem("hn_done"), sem("t_mm"), sem("hi_out"), sem("lo_out")
        f1_mm, gelu_out, f2_mm, x_out, mb2_done = (
            sem("f1_mm"), sem("gelu_out"), sem("f2_mm"), sem("x_out"), sem("mb2_done"))
        xn_in = [sem(f"xn_in{i}") for i in range(4)]
        x_st = [sem(f"x_st{i}") for i in range(2)]
        dve_own, act_own, pool_own = sem("dve_own"), sem("act_own"), sem("pool_own")

        source = [x[0], x[1], between[0], between[1]]
        target = [between[0], between[1], out[0], out[1]]

        def tile_of(j, r):
            t = 2 * j + r // 2
            return t * -1 + (TILES - 1) if r % 2 else t

        def rows(dram, h0, n):
            return dram[bass.ds(h0, n), :, :].rearrange("h w c -> w h c")

        block = ctx.enter_context(nc.Block())

        def guess(chain, m2, v, y, signal=None):
            eng = chain.eng
            chain.add(eng.tensor_scalar(v, m2, -0.5 / C, -0.5 * LN_EPS, ALU.mult, ALU.add))
            chain.settle()
            ins = eng.tensor_scalar(y.bitcast(I32), v.bitcast(I32), -0.5, MAGIC, ALU.mult, ALU.add)
            if signal is None:
                chain.add(ins)
            else:
                ins.then_inc(signal, 1)

        def newton(chain, v, y, t, half3, signal=None):
            eng = chain.eng
            for step in range(3):
                for dst, a, b, op in ((t, y, y, ALU.mult), (t, t, v, ALU.mult), (t, t, half3, ALU.add)):
                    chain.add(eng.tensor_tensor(dst, a, b, op))
                    chain.settle()
                ins = eng.tensor_tensor(y, y, t, ALU.mult)
                if step == 2 and signal is not None:
                    ins.then_inc(signal, 1)
                else:
                    chain.add(ins)
                    if step < 2:
                        chain.settle()

        def place(c):
            return c % HALF, c // HALF

        def evict_a(copy, q, cg, r):
            dst = spec[:, :, :, bass.ds(GROUP * cg, GROUP), q].rearrange("p k r c -> p (k r) c")
            return copy(dst, ps[:, 2 + r].rearrange("p (i k) -> p k i", i=GROUP))

        def evict_v(copy, cg, r):
            return copy(zbuf[:, 0:H, bass.ds(GROUP * cg, GROUP)], ps[:, r].rearrange("p (i h) -> p h i", i=GROUP))

        @block.sync
        def _(sp):
            def load_spectral(layer):
                p = params[layer]
                sp.dma_start(wraw[:, :, :, :, :], p["blocks"]).then_inc(spec_in, 16)
                sp.dma_start(vectors[:, 0:3, :], p["vectors"]).then_inc(spec_in, 16)
                sp.dma_start(b2rep[:, :, :, :], p["b2"].unsqueeze(0).to_broadcast([P, 2, 2, HALF])).then_inc(spec_in, 16)
                sp.dma_start(betarow[0:1, :], p["n1_b"]).then_inc(spec_in, 16)

            def load_gain(layer):
                sp.dma_start(gain1[:, :], params[layer]["n1_g"].to_broadcast([P, C])).then_inc(gain_in, 16)

            def load_mlp(layer):
                p = params[layer]
                sp.dma_start(mw1raw[:, :], p["mw1"]).then_inc(mlp_in, 16)
                sp.dma_start(columns[:, :], p["columns"]).then_inc(mlp_in, 16)
                sp.dma_start(mw2[:, :, :], p["mw2"].rearrange("(m k) c -> k m c", m=CHUNKS)).then_inc(mlp_in, 16)
                sp.dma_start(mb2rep[:, :], p["mb2"].to_broadcast([P, C])).then_inc(mlp_in, 16)

            n = PB * ROWS
            sp.dma_start(resid[:, 0:n, :], rows(source[0], 0, n)).then_inc(x_in[0], 16)
            sp.dma_start(cst[:, :], consts).then_inc(cst_in, 16)
            load_spectral(0)
            load_gain(0)
            for b in range(1, TILES // PB):
                sp.dma_start(resid[:, n * b:n * b + n, :], rows(source[0], n * b, n)).then_inc(x_in[b], 16)

            for s, (layer, _) in enumerate(STEPS):
                last = s == len(STEPS) - 1
                sp.wait_ge(ih_mm, CGROUPS * (s + 1))
                load_mlp(layer)
                if not last and STEPS[s + 1][0] != layer:
                    sp.wait_ge(r_done, TILES * (s + 1))
                    load_gain(layer + 1)
                    load_spectral(layer + 1)
                if s:
                    for i in range(2):
                        sp.wait_ge(x_st[i], 16 * (TILES // 2) * s)

                def load(j, r):
                    sp.wait_ge(r_done, TILES * (s + 1) + 4 * j + r - 3)
                    sp.dma_start(xnext[:, r], rows(source[s + 1], tile_of(j, r) * ROWS, ROWS)).then_inc(xn_in[r], 16)

                def store(j, r):
                    sp.wait_ge(x_out, X_CREDIT + TILES * s + 4 * j + r + 1)
                    sp.dma_start(rows(target[s], tile_of(j, r) * ROWS, ROWS), xout[:, r % 2]).then_inc(
                        x_st[r % 2], 16)

                if not last:
                    for r in range(4):
                        load(0, r)
                    with sp.Fori(1, TILES // 4) as j:
                        for r in range(4):
                            store(j - 1, r)
                            load(j, r)
                    for r in range(4):
                        store(TILES // 4 - 1, r)
                else:
                    with sp.Fori(0, TILES // 4) as j:
                        for r in range(4):
                            store(j, r)
            for i in range(2):
                sp.wait_ge(x_st[i], 16 * (TILES // 2) * len(STEPS))

        @block.tensor
        def _(pe):
            def dc_bias(n):
                pe.wait_ge(spec_built, n + 1)
                if n:
                    pe.wait_ge(x_out, X_CREDIT + TILES * IMAGES * n)
                for q in range(2):
                    for kind in range(2):
                        mm = pe.matmul(ps[:, 7, q:q + 1], w1s[0:HALF, kind, q].rearrange("p r c -> p (r c)"),
                                       beta64[0:HALF, q:q + 1], start=(q == 0 and kind == 0),
                                       stop=(kind == 1), skip_group_check=True)
                mm.then_inc(dc_mm, 1)

            def dft_w(s):
                pe.wait_ge(z_dve, Z_DVE0 + TILES * s)
                pe.wait_ge(z_act, PRO_ACT * (TILES // PB))
                for cg in range(CGROUPS):
                    if cg >= 4:
                        pe.wait_ge(a_dve if cg % 2 else a_act, CGROUPS // 2 * s + (cg - 4) // 2 + 1)
                    for i in range(GROUP):
                        mm = pe.matmul(ps[:, 2 + cg % 4, P * i:P * i + P], zbuf[:, 0:H, GROUP * cg + i], FW,
                                       start=True, stop=True)
                    mm.then_inc(s1_mm, 1)

            def dft_h(s, n):
                b, q = n // 2, n % 2
                if n >= 2:
                    pe.wait_ge(g_out, 2 * BATCHES * s + n - 1)
                for i in range(GROUP):
                    mm = pe.matmul(ps[:, q, P * i:P * i + P],
                                   spec[:, GROUP * b + i, :, :, q].rearrange("p r c -> p (r c)"), CAS,
                                   start=True, stop=True)
                mm.then_inc(s2_mm, 1)

            def mix1(s, n):
                b, q = n // 2, n % 2
                if b < BATCHES:
                    pe.wait_ge(g_out, 2 * BATCHES * s + n + 1)
                if n >= 2:
                    pe.wait_ge(o_out, UNITS * s + n - 1)

                def both(dst, src, w_plus, w_minus, start):
                    pe.matmul(dst, w_plus, src, start=start, stop=False, skip_group_check=True)
                    pe.matmul(dst[:, 1:P], w_minus, src[:, P - 1:0:-1], start=False, stop=False,
                              skip_group_check=True)
                    return pe.matmul(dst[:, 0:1], w_minus, src[:, 0:1], start=False, stop=True,
                                     skip_group_check=True)

                plus, minus, edge = (w1s[:, i, q].rearrange("p r c -> p (r c)") for i in range(3))
                if b == BATCHES:
                    dst = ps[:, 2 + q, 0:P].rearrange("p (k j) -> p k j", j=1)
                    mm = both(dst, nyq[HALF:P, q].rearrange("p (k j) -> p k j", j=1), edge[HALF:P], plus[HALF:P], True)
                else:
                    dst = ps[:, 2 + q].rearrange("p (k j) -> p k j", j=GROUP)
                    src = gsb[:, q]
                    if b:
                        mm = both(dst, src, plus, minus, True)
                    else:
                        both(dst[:, :, 1:], src[:, :, 1:], plus, minus, True)
                        both(dst[:, :, 0:1], src[0:HALF, :, 0:1], plus[0:HALF], minus[0:HALF], False)
                        mm = pe.matmul(ps[:, 2 + q, 0:1], IDENT, dcbias[:, q:q + 1], start=False, stop=True,
                                       skip_group_check=True)
                mm.then_inc(m1_mm, 1)

            def mix2(s, n):
                b, q = n // 2, n % 2
                kws = GROUP if b < BATCHES else 1
                pe.wait_ge(o_out, UNITS * s + n + 1)
                if n >= 2:
                    pe.wait_ge(v_out, UNITS * s + n - 1)
                src = osb[:, q].rearrange("p k j -> p (k j)")
                for i in range(kws):
                    mm = pe.matmul(ps[:, 4 + q, P * i:P * i + P], src[:, i:i + (P - 1) * kws + 1:kws],
                                   w2s[:, q].rearrange("p r c -> p (r c)"), start=True, stop=True)
                mm.then_inc(m2_mm, 1)

            def filter_(s):
                pe.wait_ge(a_act, CGROUPS // 2 * (s + 1))
                pe.wait_ge(a_dve, CGROUPS // 2 * (s + 1))
                pe.wait_ge(x_out, X_CREDIT + TILES * s)
                pe.wait_ge(spec_done, 1 + s // IMAGES)
                dft_h(s, 0)
                dft_h(s, 1)
                mix1(s, 0)
                for n in range(UNITS):
                    if n + 2 < 2 * BATCHES:
                        dft_h(s, n + 2)
                    if n + 1 < UNITS:
                        mix1(s, n + 1)
                    mix2(s, n)

            def idft_h(s):
                pe.wait_ge(t_edge, s + 1)
                for i, m in enumerate((REVERSE, IDENT)):
                    mm = pe.matmul(ps[:, 6, 0:2 * C], m, tedge[:, i].rearrange("p k c -> p (k c)"),
                                   start=(i == 0), stop=(i == 1))
                mm.then_inc(x_mm, 1)
                pe.wait_ge(y_done, (UNITS + 1) * (s + 1))
                for cg in range(CGROUPS):
                    if cg >= 4:
                        pe.wait_ge(v_dve if cg % 2 else v_act, CGROUPS // 2 * s + (cg - 4) // 2 + 1)
                    for i in range(GROUP):
                        ch, q = place(GROUP * cg + i)
                        mm = pe.matmul(ps[:, cg % 4, P * i:P * i + P],
                                       spec[:, :, :, ch, q].rearrange("p k r -> p (k r)"), CAS, start=True, stop=True)
                    mm.then_inc(ih_mm, 1)

            def mlp_bias(s):
                pe.wait_ge(mlp_in, MLP_IN * (s + 1))
                for m in range(CHUNKS):
                    mm = pe.matmul(ps[:, 6, m:m + 1], mw1raw[:, P * m:P * m + P], beta2[:, 0:1],
                                   start=(m == 0), stop=(m == CHUNKS - 1), skip_group_check=True)
                mm.then_inc(mlp_b_mm, 1)

            def idft_w(s, j, r):
                n = 4 * j + r
                pe.wait_ge(h2_done, TILES * s + n)
                t = tile_of(j, r)
                src = zbuf[:, bass.ds(ROWS * t, ROWS), :]
                back = zbuf[:, bass.ds(t * -ROWS + (H + 1 - ROWS), ROWS), :]
                pe.matmul(ps[:, 7], D1, src, start=True, stop=False)
                turned = ps[:, 7].rearrange("p (h c) -> p h c", h=ROWS)[:, ::-1]
                pe.matmul(turned, D2, back, start=False, stop=True).then_inc(iw_mm, 1)

            def turn(s, n, r):
                pe.wait_ge(hn_done, TILES * s + n + 1)
                pe.wait_ge(lo_out, TILES * s + n)
                for i in range(ROWS):
                    mm = pe.transpose(ps[:, 6, P * i:P * i + P], hn[:, r % 2, i, :], IDENT)
                mm.then_inc(t_mm, 1)

            def fc1(s, n, r, m):
                if m == 0:
                    pe.wait_ge(lo_out, TILES * s + n + 1)
                if isinstance(n, int) and n == 0:
                    pass
                else:
                    pe.wait_ge(gelu_out, CHUNKS * TILES * s + CHUNKS * n + m - 3)
                h, l = mw1h[:, P * m:P * m + P], mw1l[:, P * m:P * m + P]
                pe.matmul(ps[:, 2 + m], h, hth[:, r % 2, :], start=True, stop=False)
                pe.matmul(ps[:, 2 + m], h, htl[:, r % 2, :], start=False, stop=False)
                pe.matmul(ps[:, 2 + m], l, hth[:, r % 2, :], start=False, stop=True).then_inc(f1_mm, 1)

            def fc2(s, n, r, m):
                pe.wait_ge(gelu_out, CHUNKS * TILES * s + CHUNKS * n + m + 1)
                if m == 0:
                    pe.wait_ge(x_out, X_CREDIT + TILES * s + n - 1)
                for i in range(ROWS):
                    mm = pe.matmul(ps[:, r % 2, P * i:P * i + P], gel[:, r % 2, m, P * i:P * i + P], mw2[:, m, :],
                                   start=(m == 0 and i == 0), stop=(m == CHUNKS - 1), skip_group_check=True)
                if m == CHUNKS - 1:
                    mm.then_inc(f2_mm, 1)

            def mlp(s):
                pe.wait_ge(v_wrap, s + 1)
                idft_w(s, 0, 0)
                mlp_bias(s)
                idft_w(s, 0, 1)
                pe.wait_ge(mlp_b, s + 1)
                turn(s, 0, 0)
                idft_w(s, 0, 2)
                turn(s, 1, 1)
                pe.wait_ge(mlp_w, s + 1)
                for m in range(CHUNKS):
                    fc1(s, 0, 0, m)

                def tile(j, r, iw=True, tr=True, nx=True):
                    n = 4 * j + r
                    if iw:
                        idft_w(s, j + (r + 3) // 4, (r + 3) % 4)
                    if tr:
                        turn(s, n + 2, r + 2)
                    for m in range(CHUNKS):
                        if nx:
                            fc1(s, n + 1, r + 1, m)
                        fc2(s, n, r, m)

                with pe.Fori(0, TILES // 4 - 1) as j:
                    for r in range(4):
                        tile(j, r)
                for r in range(4):
                    n = TILES - 4 + r
                    tile(TILES // 4 - 1, r, n + 3 < TILES, n + 2 < TILES, n + 1 < TILES)

            pe.wait_ge(cst_in, 16)
            for s in range(len(STEPS)):
                if s % IMAGES == 0:
                    dc_bias(s // IMAGES)
                dft_w(s)
                filter_(s)
                idft_h(s)
                mlp(s)

        @block.scalar
        def _(act):
            def a_out(s, q, j, r):
                act.wait_ge(s1_mm, CGROUPS * s + CGROUPS // 2 * q + 4 * j + r + 1)
                evict_a(act.copy, q, 4 * j + r, r).then_inc(a_act, 1)

            def g_copy(s, n, q, first=False):
                act.wait_ge(s2_mm, 2 * BATCHES * s + n + 1)
                if first:
                    act.copy(nyq[HALF:P, q], ps[HALF:P, q, 0:P])
                else:
                    act.wait_ge(m1_mm, UNITS * s + n - 1)
                src = ps[:, q].rearrange("p (j k) -> p k j", j=GROUP)
                act.copy(gsb[:, q], src).then_inc(g_out, 1)

            def o_relu(s, n, q, kws=GROUP, first=False):
                act.wait_ge(m1_mm, UNITS * s + n + 1)
                if not first:
                    act.wait_ge(m2_mm, UNITS * s + n - 1)
                dst = osb[:, q].rearrange("p k j -> p (k j)")[:, 0:P * kws]
                act.activation(dst, ps[:, 2 + q, 0:P * kws], ACT.Relu, bias=b1v[:, q:q + 1]).then_inc(o_out, 1)

            def v_out_(s, cg, r):
                act.wait_ge(ih_mm, CGROUPS * s + cg + 1)
                evict_v(act.copy, cg, r).then_inc(v_act, 1)

            def hi(s, n, r):
                act.wait_ge(t_mm, TILES * s + n + 1)
                act.copy(hth[:, r % 2, :], ps[:, 6]).then_inc(hi_out, 1)

            def gelu(s, n, r):
                for m in range(CHUNKS):
                    act.wait_ge(f1_mm, CHUNKS * TILES * s + CHUNKS * n + m + 1)
                    if m == 0 and not (isinstance(n, int) and n < 2):
                        act.wait_ge(f2_mm, TILES * s + n - 1)
                    act.activation(gel[:, r % 2, m, :], ps[:, 2 + m], ACT.Gelu, bias=mb1f[:, m:m + 1]).then_inc(
                        gelu_out, 1)

            for b in range(TILES // PB):
                act.wait_ge(st_pro, b + 1)
                for t in range(PB - PRO_ACT, PB):
                    for i in range(ROWS):
                        h = (PB * b + t) * ROWS + i
                        ins = act.activation(zbuf[:, h, :], resid[:, h, :], ACT.Identity,
                                             bias=pnm[:, h:h + 1], scale=prs[:, h:h + 1])
                    ins.then_inc(z_act, 1)
            for s in range(len(STEPS)):
                if s:
                    act.wait_ge(r_done, TILES * (s + 1))
                for q in range(2):
                    with act.Fori(0, CGROUPS // 8) as j:
                        for r in (0, 2):
                            a_out(s, q, j, r)
                act.wait_ge(r_done, TILES * (s + 1))
                g_copy(s, 0, 0, first=True)

                def batch(b, first=False, last=False):
                    g_copy(s, 2 * b + 1, 1, first=first)
                    o_relu(s, 2 * b, 0, first=first)
                    if not last:
                        g_copy(s, 2 * b + 2, 0)
                    o_relu(s, 2 * b + 1, 1, first=first)

                batch(0, first=True)
                with act.Fori(1, BATCHES - 1) as b:
                    batch(b)
                batch(BATCHES - 1, last=True)
                o_relu(s, UNITS - 2, 0, kws=1)
                o_relu(s, UNITS - 1, 1, kws=1)
                with act.Fori(0, CGROUPS // 4) as j:
                    for r in (0, 2):
                        v_out_(s, 4 * j + r, r)
                hi(s, 0, 0)
                act.wait_ge(mlp_b, s + 1)
                for r in range(4):
                    hi(s, r + 1, r + 1)
                    gelu(s, r, r)
                with act.Fori(1, TILES // 4 - 1) as j:
                    for r in range(4):
                        hi(s, 4 * j + r + 1, r + 1)
                        gelu(s, 4 * j + r, r)
                for r in range(4):
                    n = TILES - 4 + r
                    if n + 1 < TILES:
                        hi(s, n + 1, r + 1)
                    gelu(s, n, r)

        @block.vector
        def _(dve):
            own = Chain(dve, dve_own)

            def build_spectral(n):
                dve.wait_ge(spec_in, SPEC_IN * (n + 1))
                if n:
                    dve.wait_ge(ih_mm, CGROUPS * n * IMAGES)
                re, im = slice(0, HALF), slice(HALF, P)
                own.add(dve.tensor_tensor(wsum[:, 0], wraw[:, 0, 0], wraw[:, 0, 1], ALU.add))
                own.add(dve.tensor_tensor(wsum[:, 1], wraw[:, 0, 0], wraw[:, 0, 1], ALU.subtract))
                own.settle()
                jobs = [(w1s[:, 0], wsum, [(re, 0, 0, 2), (re, 1, 1, 3), (im, 0, 1, 2), (im, 1, 0, 2)]),
                        (w1s[:, 1], wsum, [(re, 0, 1, 2), (re, 1, 0, 2), (im, 0, 0, 3), (im, 1, 1, 2)]),
                        (w1s[:, 2], wsum, [(im, 0, 0, 2), (im, 1, 1, 3), (re, 0, 0, 2), (re, 1, 1, 3)]),
                        (w2s[:, :], wraw[:, 1], [(re, 0, 0, 0), (re, 1, 1, 0), (im, 0, 1, 1), (im, 1, 0, 0)])]
                for dst, raw, parts in jobs:
                    for part, col, j, sign in parts:
                        for q in range(2):
                            src = raw[part, j, q, :].unsqueeze(1).to_broadcast([HALF, BLOCKS, BLOCK])
                            m = mask[part, sign, :].unsqueeze(2).to_broadcast([HALF, BLOCKS, BLOCK])
                            to = dst[part, q, col, :].rearrange("p (b o) -> p b o", b=BLOCKS)
                            own.add(dve.tensor_tensor(to, src, m, ALU.mult))
                own.settle()
                dve.nop().then_inc(spec_built, 1)
                dve.wait_ge(dc_mm, n + 1)
                own.add(dve.tensor_scalar(dcbias[:, :], ps[:, 7, 0:2], DC, None, ALU.mult))
                own.add(dve.tensor_scalar(betarow[0:1, :], betarow[0:1, :], DC, None, ALU.mult))
                for q in range(2):
                    for kind in range(3):
                        t = w1s[:, kind, q].rearrange("p r c -> p (r c)")
                        own.add(dve.tensor_scalar(t, t, gain64[:, q:q + 1], None, ALU.mult))
                own.settle()
                dve.nop().then_inc(spec_done, 1)

            def bn(tile, to):
                for i in range(ROWS // 2):
                    src = tile[:, 2 * i:2 * i + 2, :].rearrange("p h c -> p c h")
                    ins = dve.bn_stats(to[:, 2 * i:2 * i + 2, :].rearrange("p h k -> p (h k)"), src)
                return ins

            own.add(dve.memset(p15[:, :], 1.5))
            dve.wait_ge(cst_in, 16)
            dve.nop().then_inc(x_out, X_CREDIT)
            build_spectral(0)
            for b in range(TILES // PB):
                dve.wait_ge(x_in[b], 16)
                h0 = PB * ROWS * b
                own_rows = slice(h0, h0 + PB * ROWS)
                for t in range(PB):
                    h = h0 + ROWS * t
                    own.add(bn(resid[:, h:h + ROWS, :], pst[:, h:h + ROWS, :]))
                own.settle()
                guess(own, pst[:, own_rows, 2], pva[:, :], prs[:, own_rows])
                own.settle()
                newton(own, pva[:, :], prs[:, own_rows], pn0[:, :], p15[:, :])
                own.settle()
                own.add(dve.scalar_tensor_tensor(pnm[:, own_rows], pst[:, own_rows, 1], -1.0, prs[:, own_rows],
                                                 ALU.mult, ALU.mult))
                own.settle()
                dve.nop().then_inc(st_pro, 1)
                for t in range(PB - PRO_ACT):
                    for i in range(ROWS):
                        h = h0 + ROWS * t + i
                        ins = dve.tensor_scalar(zbuf[:, h, :], resid[:, h, :], pst[:, h, 1:2], prs[:, h:h + 1],
                                                ALU.subtract, ALU.mult)
                    ins.then_inc(z_dve, 1)

            def a_out(s, q, j, r):
                dve.wait_ge(s1_mm, CGROUPS * s + CGROUPS // 2 * q + 4 * j + r + 1)
                evict_a(dve.tensor_copy, q, 4 * j + r, r).then_inc(a_dve, 1)

            def shrink(s, n, b, q, kws=GROUP):
                dve.wait_ge(m2_mm, UNITS * s + n + 1)
                bias = b2rep[:, q].rearrange("p r c -> p (r c)").unsqueeze(1).to_broadcast([P, kws, P])
                v = vsb[:, q].rearrange("p j r c -> p j (r c)")[:, 0:kws]
                cl = csb[:, q].rearrange("p j r c -> p j (r c)")[:, 0:kws]
                src = ps[:, 4 + q, 0:P * kws].rearrange("p (j k) -> p j k", j=kws)
                dve.tensor_tensor(v, src, bias, ALU.add).then_inc(v_out, 1)
                dve.wait_ge(v_out, UNITS * s + n + 1)
                own.add(dve.tensor_scalar(cl, v, -LAM, LAM, ALU.max, ALU.min))
                own.settle()
                v, cl = vsb[:, q], csb[:, q]
                if kws == 1 or isinstance(b, int) and b == 0:
                    edge = yedge[:, 0 if kws > 1 else 1, :, :, q]
                    ins = dve.tensor_tensor(edge, v[:, 0], cl[:, 0], ALU.subtract)
                    if kws == 1:
                        ins.then_inc(y_done, 1)
                        return
                    own.add(ins)
                    dst, v, cl = spec[:, 1:GROUP, :, :, q], v[:, 1:], cl[:, 1:]
                else:
                    dst = spec[:, bass.ds(GROUP * b, GROUP), :, :, q]
                dve.tensor_tensor(dst, v, cl, ALU.subtract).then_inc(y_done, 1)

            def edges(s):
                dve.wait_ge(y_done, (UNITS + 1) * s + UNITS)
                own.settle()
                dve.wait_ge(spec_done, 1 + s // IMAGES)
                shift = yedge[0:1, 0, 0].rearrange("p c q -> p q c")
                own.add(dve.tensor_tensor(shift, shift, betarow[0:1, :].rearrange("p (q c) -> p q c", q=2), ALU.add))
                own.settle()
                for i, op in enumerate((ALU.add, ALU.subtract)):
                    ins = dve.tensor_tensor(tedge[:, i], yedge[:, :, 0].rearrange("p k c q -> p k (c q)"),
                                            yedge[:, :, 1].rearrange("p k c q -> p k (c q)"), op)
                ins.then_inc(t_edge, 1)
                dve.wait_ge(x_mm, s + 1)
                dve.tensor_scalar(spec[:, 0].rearrange("p r c q -> p (r c q)"), ps[:, 6, 0:2 * C], 0.5, None,
                                  ALU.mult).then_inc(y_done, 1)

            def v_out_(s, cg, r):
                dve.wait_ge(ih_mm, CGROUPS * s + cg + 1)
                evict_v(dve.tensor_copy, cg, r).then_inc(v_dve, 1)

            def split_weights(s):
                dve.wait_ge(mlp_in, MLP_IN * (s + 1))
                own.add(dve.tensor_scalar(mw1h[:, :], mw1raw[:, :], gain2[:, 0:1], None, ALU.mult))
                own.settle()
                dve.scalar_tensor_tensor(mw1l[:, :], mw1raw[:, :], gain2[:, 0:1], mw1h[:, :].bitcast(F32),
                                         ALU.mult, ALU.subtract).then_inc(mlp_w, 1)
                dve.wait_ge(mlp_b_mm, s + 1)
                dve.tensor_tensor(mb1f[:, :], ps[:, 6, 0:CHUNKS], mb1[:, :], ALU.add).then_inc(mlp_b, 1)

            def rows_of(buf, j, r, n=ROWS, i=0):
                return buf[:, bass.ds(ROWS * tile_of(j, r) + i, n), :].rearrange("p h c -> p (h c)")

            def h2(s, j, r):
                dve.wait_ge(iw_mm, TILES * s + 4 * j + r + 1)
                t = rows_of(resid, j, r)
                dve.tensor_tensor(t, ps[:, 7], t, ALU.add).then_inc(h2_done, 1)

            def statistics(s, n, j, r, second, first):
                if second:
                    ins = bn(resid[:, bass.ds(ROWS * tile_of(j, r), ROWS), :], stats[:, r % 4, 0:ROWS, :])
                if first:
                    at_ = (r - LAG) % 4
                    dve.wait_ge(xn_in[at_], 16 * (TILES // 4 * s + j + (r - LAG) // 4 + 1))
                    ins = bn(xnext[:, at_], stats[:, r % 4, ROWS:2 * ROWS, :])
                own.add(ins)
                own.settle()
                lo_, hi_ = 0 if second else ROWS, 2 * ROWS if first else ROWS
                guess(own, stats[:, r % 4, lo_:hi_, 2], var[:, r % 4, lo_:hi_], rstd[:, r % 4, lo_:hi_], st_done)

            def lower(s, n, r, start):
                dve.wait_ge(hi_out, TILES * s + n + 1)
                if not start:
                    dve.wait_ge(f1_mm, CHUNKS * (TILES * s + n - 1))
                dve.tensor_tensor(htl[:, r % 2, :], ps[:, 6], hth[:, r % 2, :].bitcast(F32),
                                  ALU.subtract).then_inc(lo_out, 1)

            def x_new(s, j, r):
                n = 4 * j + r
                dve.wait_ge(f2_mm, TILES * s + n + 1)
                dve.wait_ge(mb2_done, TILES * s + n + 1)
                if not (isinstance(j, int) and s == 0 and n < 2):
                    dve.wait_ge(x_st[r % 2], 16 * (TILES // 2 * s + 2 * j + r // 2))
                t = rows_of(resid, j, r)
                dve.tensor_tensor(xout[:, r % 2].rearrange("p h c -> p (h c)"), ps[:, r % 2], t,
                                  ALU.add).then_inc(x_out, 1)

            def z_new(s, j, r):
                slot = (r + LAG) % 4
                for i in range(ROWS):
                    ins = dve.tensor_scalar(rows_of(zbuf, j, r, 1, i), xnext[:, r, i, :],
                                            stats[:, slot, ROWS + i, 1:2], rstd[:, slot, ROWS + i:ROWS + i + 1],
                                            ALU.subtract, ALU.mult)
                ins.then_inc(z_dve, 1)

            def normal(s, j, r):
                n = 4 * j + r
                dve.wait_ge(rs_done, STATS * s + n + 1)
                if not (isinstance(j, int) and n < 2):
                    dve.wait_ge(t_mm, TILES * s + n - 1)
                for i in range(ROWS):
                    ins = dve.tensor_scalar(hn[:, r % 2, i, :], rows_of(resid, j, r, 1, i),
                                            stats[:, r % 4, i, 1:2], rstd[:, r % 4, i:i + 1],
                                            ALU.subtract, ALU.mult)
                ins.then_inc(hn_done, 1)

            for s in range(len(STEPS)):
                last = s == len(STEPS) - 1
                if s:
                    dve.wait_ge(r_done, TILES * (s + 1))
                for q in range(2):
                    with dve.Fori(0, CGROUPS // 8) as j:
                        for r in (1, 3):
                            a_out(s, q, j, r)
                for q in range(2):
                    shrink(s, q, 0, q)
                with dve.Fori(1, BATCHES) as b:
                    own.enter(b, 2, 1)
                    for q in range(2):
                        shrink(s, 2 * b + q, b, q)
                own.leave(BATCHES)
                for q in range(2):
                    shrink(s, UNITS - 2 + q, BATCHES, q, kws=1)
                edges(s)
                with dve.Fori(0, CGROUPS // 4) as j:
                    for r in (1, 3):
                        v_out_(s, 4 * j + r, r)
                dve.wait_ge(v_act, CGROUPS // 2 * (s + 1))
                dve.wait_ge(v_dve, CGROUPS // 2 * (s + 1))
                dve.tensor_copy(zbuf[:, H, :], zbuf[:, 0, :]).then_inc(v_wrap, 1)

                def tile(j, r):
                    n = 4 * j + r
                    known = n if isinstance(j, int) else 8
                    nxt = not last
                    main = known < TILES
                    if main:
                        h2(s, j, r)
                        dve.wait_ge(h2_done, TILES * s + n + 1)
                    if 1 <= known <= TILES:
                        lower(s, n - 1, (r - 1) % 4, known < 3)
                    if main or nxt and known < TILES + LAG:
                        statistics(s, n, j, r, main, nxt and known >= LAG)
                    if known >= 4 and known < TILES + 4:
                        x_new(s, j - 1, r)
                    if nxt and LAG + 1 <= known <= TILES + LAG:
                        if not main:
                            dve.wait_ge(rs_done, STATS * s + n)
                        z_new(s, j + (r - LAG - 1) // 4, (r - LAG - 1) % 4)
                    if main:
                        normal(s, j, r)

                for n in range(8):
                    if n == 1:
                        split_weights(s)
                    tile(n // 4, n % 4)
                with dve.Fori(2, TILES // 4) as j:
                    own.enter(j, 4 * 2, 2)
                    for r in range(4):
                        tile(j, r)
                own.leave(TILES // 4)
                for r in range(4):
                    tile(TILES // 4, r)
                if s + 1 < len(STEPS) and STEPS[s + 1][0] != STEPS[s][0]:
                    build_spectral(STEPS[s + 1][0])

        @block.gpsimd
        def _(pool):
            own = Chain(pool, pool_own)
            pool.memset(c15[:, :], 1.5).then_inc(pool_own, 1)
            own.n += 1

            def residual(h0, xtile, tmp, count):
                z = zbuf[:, h0, :]
                g = gain1[:, :].unsqueeze(1).to_broadcast([P, ROWS, C])
                pool.tensor_tensor(tmp, z, g, ALU.mult).then_inc(gz_done, 1)
                pool.wait_ge(gz_done, count)
                pool.tensor_tensor(resid[:, h0, :], xtile, tmp, ALU.add).then_inc(r_done, 1)

            pool.wait_ge(gain_in, 16)
            done = [0, 0]
            for t in range(TILES):
                who = 0 if t % PB < PB - PRO_ACT else 1
                done[who] += 1
                pool.wait_ge((z_dve, z_act)[who], done[who])
                if t >= 2:
                    pool.wait_ge(r_done, t - 1)
                h = slice(ROWS * t, ROWS * t + ROWS)
                residual(h, resid[:, h, :], xout[:, t % 2], t + 1)

            for s in range(len(STEPS)):
                last = s == len(STEPS) - 1
                if not last and STEPS[s + 1][0] != STEPS[s][0]:
                    pool.wait_ge(gain_in, 16 * 2)

                pool.wait_ge(mlp_in, MLP_IN * (s + 1))

                def inverse_std(s, n, r, lo_, hi_):
                    pool.wait_ge(st_done, STATS * s + n + 1)
                    newton(own, var[:, r % 4, lo_:hi_], rstd[:, r % 4, lo_:hi_], nt0[:, lo_:hi_], c15[:, lo_:hi_],
                           signal=rs_done)

                def bias(s, j, r):
                    pool.wait_ge(hn_done, TILES * s + 4 * j + r + 1)
                    t = resid[:, bass.ds(ROWS * tile_of(j, r), ROWS), :]
                    b = mb2rep[:, :].unsqueeze(1).to_broadcast([P, ROWS, C])
                    pool.tensor_tensor(t, t, b, ALU.add).then_inc(mb2_done, 1)

                def tile(j, r):
                    n = 4 * j + r
                    known = n if isinstance(j, int) else 8
                    nxt = not last
                    main = known < TILES
                    if main or nxt and known < TILES + LAG:
                        inverse_std(s, n, r, 0 if main else ROWS, 2 * ROWS if nxt and known >= LAG else ROWS)
                    if 1 <= known <= TILES:
                        bias(s, j + (r - 1) // 4, (r - 1) % 4)
                    if nxt and known >= 5:
                        m, at_ = n - 5, (r - 5) % 4
                        pool.wait_ge(z_dve, Z_DVE0 + TILES * s + m + 1)
                        pool.wait_ge(x_out, X_CREDIT + TILES * s + m + 1)
                        pool.wait_ge(r_done, TILES * (s + 1) + m - 1)
                        residual(bass.ds(ROWS * tile_of(j + (r - 5) // 4, at_), ROWS), xnext[:, at_],
                                 gz[:, at_ % 2], TILES * (s + 1) + m + 1)

                per = 4 * 11
                for n in range(8):
                    tile(n // 4, n % 4)
                with pool.Fori(2, TILES // 4) as j:
                    own.enter(j, per, 2)
                    for r in range(4):
                        tile(j, r)
                own.leave(TILES // 4)
                for n in range(TILES, TILES + 5):
                    tile(n // 4, n % 4)

    return nc


_PARAMS = ["n1_g", "n1_b", "n2_g", "n2_b", "w1", "b1", "w2", "b2", "mw1", "mb1", "mw2", "mb2"]


def kernel(**inputs):
    import numpy as _np
    import concourse.bacc as _bacc
    from concourse import mybir as _mybir
    from concourse.bass_utils import run_bass_kernel_spmd as _run

    nc = _bacc.Bacc("TRN2", target_bir_lowering=False, num_devices=1)
    arrays = {}

    def given(name, a):
        a = _np.ascontiguousarray(a)
        arrays[f"in_{name}_dram"] = a
        return nc.dram_tensor(f"in_{name}_dram", a.shape, _mybir.dt.from_np(a.dtype), kind="ExternalInput").ap()

    def laid_out(layer):
        p = {n: _np.asarray(inputs[f"L{layer}_conv_{n}"]) for n in _PARAMS}

        def twice(a):
            return _np.concatenate([a, a], 0)

        def by_row(w):
            return w.reshape(2, 2, HALF, BLOCK).transpose(2, 0, 1, 3)

        b1 = p["b1"].reshape(2, 2, HALF).transpose(0, 2, 1).reshape(P, 2)
        return {
            "blocks": twice(_np.stack([by_row(p["w1"]), by_row(p["w2"])], 1)),
            "vectors": _np.stack([twice(p["n1_g"].reshape(2, HALF).T), twice(p["n1_b"].reshape(2, HALF).T), b1], 1),
            "b2": p["b2"].reshape(2, 2, HALF).transpose(1, 0, 2),
            "n1_b": p["n1_b"][None],
            "n1_g": p["n1_g"][None],
            "mw1": p["mw1"],
            "mw2": p["mw2"],
            "mb2": p["mb2"][None],
            "columns": _np.concatenate([p["n2_g"][:, None], p["n2_b"][:, None], p["mb1"].reshape(CHUNKS, P).T], 1),
        }

    x = given("x", inputs["x"])
    consts = given("consts", dft_constants())
    params = [{n: given(f"L{layer}_{n}", a) for n, a in laid_out(layer).items()} for layer in range(LAYERS)]
    out = nc.dram_tensor("out_0_dram", (IMAGES, H, W, C), _mybir.dt.float32, kind="ExternalOutput").ap()
    afno(nc, x, consts, params, out)
    r = _run(nc, [arrays], core_ids=[0])
    return r.results[0]["out_0_dram"]
```

```python
from contextlib import ExitStack

import numpy as np

import concourse.bass as bass
from concourse import mybir

F32 = mybir.dt.float32
F32R = mybir.dt.float32r
I32 = mybir.dt.int32
ALU = mybir.AluOpType
ACT = mybir.ActivationFunctionType

P = 128
IMAGES, LAYERS = 2, 2
H = W = C = 128
HALF = C // 2
BLOCK = 16
BLOCKS = HALF // BLOCK
LATENT = 4 * C
CHUNKS = LATENT // P
KWS = W // 2
ROWS = 4
TILES = H // ROWS
TOK = ROWS * W
GROUP = 4
CGROUPS = C // GROUP
BATCHES = KWS // GROUP
UNITS = 2 * BATCHES + 2
LN_EPS = 1e-5
LAM = 0.01
DC = float(np.sqrt(H * W))
MAGIC = float(0x5F3759DF - 2 ** 22 - 2 ** 30)
STEPS = [(layer, image) for layer in range(LAYERS) for image in range(IMAGES)]
LAG = 2
PRO_ACT = 6
CONSTS = 7 * P + 2 * BLOCKS
PAIRS = TILES // 2
EVEN = KWS + 1
PB = 8
Z_DVE0 = (PB - PRO_ACT) * (TILES // PB)
SPEC_IN = 16 * 4
RAW_IN = MLP_IN = 16 * 2
Y_CREDIT = 2


def row_of():
    h = np.arange(P)
    h[:HALF], h[HALF] = np.arange(1, HALF + 1), 0
    return h


def dft_constants():
    n = np.arange(P, dtype=np.float64)
    h = row_of().astype(np.float64)
    turn = 2 * np.pi / P
    scale = 1 / np.sqrt(P)
    k = np.arange(EVEN, dtype=np.float64)
    cos = np.cos(turn * np.outer(n, k)) * scale
    sin = np.sin(turn * np.outer(n, k)) * scale
    fw = np.stack([cos[:, :KWS], -sin[:, :KWS]], 2)
    fw[:, 0, 1] = cos[:, KWS]
    fh = np.concatenate([np.cos(turn * np.outer(h, k)), np.sin(turn * np.outer(h, k[1:-1]))], 1) * scale
    k_of = np.concatenate([k, -k[1:-1]])
    ih = np.concatenate([np.cos(turn * np.outer(k_of, h[:HALF + 1])),
                         np.sin(turn * np.outer(k_of, -h[HALF + 1:]))], 1) * scale
    de = 2 * np.stack([cos, -sin], 2)[:, :KWS]
    do = 2 * np.stack([-sin, -cos], 2)[:, :KWS]
    for d in (de, do):
        d[:, 0, 0], d[:, 0, 1] = cos[:, 0], cos[:, KWS]
    reverse = (k_of[:, None] % P == -k_of[None] % P).astype(np.float64)
    block = (np.arange(P) % HALF) // BLOCK
    mask = (block[:, None] == np.arange(BLOCKS)[None]).astype(np.float64)
    parts = [fw.reshape(P, P), fh, ih, de.reshape(P, P).T, do.reshape(P, P).T, np.eye(P), reverse]
    return np.concatenate([*parts, mask, -mask], 1).astype(np.float32)


class Chain:

    def __init__(self, eng, sem):
        self.eng, self.sem, self.base, self.trip, self.n = eng, sem, 0, None, 0

    def add(self, ins):
        ins.then_inc(self.sem, 1)
        self.n += 1

    def settle(self):
        at = self.base + self.n
        self.eng.wait_ge(self.sem, at if self.trip is None else self.trip * self.per + at)

    def enter(self, trip, per, first):
        self.base, self.n, self.trip, self.per = self.base + self.n - first * per, 0, trip, per

    def leave(self, end):
        assert self.n == self.per, self.n
        self.base, self.n, self.trip = self.base + end * self.per, 0, None


def afno(nc, x, consts, params, out):
    ctx = ExitStack()
    with ctx:
        top = [(nc.sbuf_base + 63) // 64 * 64]

        def at(name, shape, offset, dtype=F32):
            return nc.alloc_sbuf_tensor_at(name, shape, dtype, offset=offset)

        def size(shape):
            return int(np.prod(shape[1:])) * 4

        def sb(name, shape, dtype=F32):
            offset = top[0]
            top[0] = (offset + size(shape) + 31) // 32 * 32
            return at(name, shape, offset, dtype)

        def sem(name):
            return ctx.enter_context(nc.semaphore(name))

        resid = sb("resid", [P, H, C])
        zbuf_at = top[0]
        zbuf = sb("zbuf", [P, H, C])
        spec_at = top[0]
        spec = sb("spec", [P, KWS, 2, HALF, 2])
        spec_end = top[0]
        cst = sb("cst", [P, CONSTS])
        FW, FH, IH, DE, DO, IDENT, REVERSE = (cst[:, i * P:(i + 1) * P] for i in range(7))
        mask = cst[:, 7 * P:].rearrange("p (s b) -> p s b", s=2)
        w1s = sb("w1s", [P, 2, 2, 2, HALF])
        w2s = sb("w2s", [P, 2, 2, HALF])
        wraw = sb("wraw", [P, 2, 2, 2, BLOCK])
        vectors = sb("vectors", [P, 4, 2])
        gain64, beta64, b1v, dcbias = (vectors[:, i, :] for i in range(4))
        b2rep = sb("b2rep", [P, 2, 2, HALF])
        betarow = sb("betarow", [P, C])
        gain1 = sb("gain1", [P, C])
        columns = sb("columns", [P, 2 + CHUNKS])
        gain2, beta2, mb1 = columns[:, 0:1], columns[:, 1:2], columns[:, 2:]
        mb1f = sb("mb1f", [P, CHUNKS])
        stats = sb("stats", [P, 2, 4 * ROWS, 3])
        rstd = sb("rstd", [P, 2, 4 * ROWS])
        var = sb("var", [P, 4 * ROWS])
        shift = sb("shift", [P, 2, 2 * ROWS])
        nt0 = sb("nt0", [P, 4 * ROWS])
        xout_at = top[0]
        xout = sb("xout", [P, 2, ROWS, C])
        assert top[0] <= nc.sbuf_usable_end, (top[0], nc.sbuf_usable_end)

        mw1raw = at("mw1raw", [P, LATENT], xout_at + size([P, ROWS, C]))
        o = zbuf_at
        gsb = at("gsb", [P, 2, P, GROUP], o); o += size(gsb.shape)
        usb = at("usb", [P, 2, P, GROUP], o); o += size(usb.shape)
        osb = at("osb", [P, 2, P, GROUP], o); o += size(osb.shape)
        vsb = at("vsb", [P, 2, GROUP, 2, HALF], o); o += size(vsb.shape)
        csb = at("csb", [P, 2, GROUP, 2, HALF], o); o += size(csb.shape)
        nyq = at("nyq", [P, 2, P], o); o += size(nyq.shape)
        yedge = at("yedge", [P, 2, 2, HALF, 2], o); o += size(yedge.shape)
        tedge = at("tedge", [P, 2, 2, C], o); o += size(tedge.shape)
        assert o <= spec_at
        o = spec_at
        xnext = at("xnext", [P, 4, ROWS, C], o); o += size(xnext.shape)
        gz = at("gz", [P, 2, ROWS, C], o); o += size(gz.shape)
        hn = at("hn", [P, 2, ROWS, C], o); o += size(hn.shape)
        hth = at("hth", [P, 2, TOK], o, F32R); o += size(hth.shape)
        htl = at("htl", [P, 2, TOK], o, F32R); o += size(htl.shape)
        gel = at("gel", [P, 2, CHUNKS, TOK], o); o += size(gel.shape)
        mw1h = at("mw1h", [P, LATENT], o, F32R); o += size(mw1h.shape)
        mw1l = at("mw1l", [P, LATENT], o, F32R); o += size(mw1l.shape)
        mw2 = at("mw2", [P, CHUNKS, C], o); o += size(mw2.shape)
        mb2rep = at("mb2rep", [P, C], o); o += size(mb2rep.shape)
        assert o <= spec_end
        pst = at("pst", [P, TILES * ROWS, 3], o); o += size(pst.shape)
        prs = at("prs", [P, TILES * ROWS], o); o += size(prs.shape)
        pnm = at("pnm", [P, TILES * ROWS], o); o += size(pnm.shape)
        pva = at("pva", [P, PB * ROWS], o); o += size(pva.shape)
        pn0 = at("pn0", [P, PB * ROWS], o); o += size(pn0.shape)
        assert o <= spec_end

        ps = ctx.enter_context(nc.psum_tensor("ps", [P, 8, 512], F32))
        between = nc.dram_tensor("between", [IMAGES, H, W, C], F32).ap()

        cst_in, mask_in = sem("cst_in"), sem("mask_in")
        x_in = [sem(f"x_in{b}") for b in range(TILES // PB)]
        spec_in, gain_in, raw_in, mlp_in = sem("spec_in"), sem("gain_in"), sem("raw_in"), sem("mlp_in")
        spec_built, dc_mm, spec_done = sem("spec_built"), sem("dc_mm"), sem("spec_done")
        st_pro, z_dve, z_act, gz_done, r_done = (sem(n) for n in ("st_pro", "z_dve", "z_act", "gz_done", "r_done"))
        s1_mm, a_act, a_dve = (sem(n) for n in ("s1_mm", "a_act", "a_dve"))
        s2_mm, m1_mm, m2_mm = sem("s2_mm"), sem("m1_mm"), sem("m2_mm")
        g_out, e_out, u_out, o_out, v_out, y_done = sem("g_out"), sem("e_out"), sem("u_out"), sem("o_out"), sem("v_out"), sem("y_done")
        t_edge, x_mm = sem("t_edge"), sem("x_mm")
        ih_mm, v_act, v_dve = sem("ih_mm"), sem("v_act"), sem("v_dve")
        mlp_w, mlp_b_mm, mlp_b = sem("mlp_w"), sem("mlp_b_mm"), sem("mlp_b")
        iw_mm, h2_done, rs_done = sem("iw_mm"), sem("h2_done"), sem("rs_done")
        hn_done, t_mm, hi_out, lo_out = sem("hn_done"), sem("t_mm"), sem("hi_out"), sem("lo_out")
        f1_mm, gelu_out, f2_mm, y_out, x_out, mb2_done = (
            sem("f1_mm"), sem("gelu_out"), sem("f2_mm"), sem("y_out"), sem("x_out"), sem("mb2_done"))
        xn_in = [sem(f"xn_in{i}") for i in range(4)]
        x_st = [sem(f"x_st{i}") for i in range(2)]
        row0_in, row0_st = sem("row0_in"), sem("row0_st")
        dve_own = sem("dve_own")

        source = [x[0], x[1], between[0], between[1]]
        target = [between[0], between[1], out[0], out[1]]

        def tile_of(j, r):
            t = 2 * j + r // 2
            return t * -1 + (TILES - 1) if r % 2 else t

        def rows(dram, h0, n):
            return dram[bass.ds(h0, n), :, :].rearrange("h w c -> w h c")

        def transfers(sp, dram, tile, j, r, done, row0, store):
            last = isinstance(j, int) and 4 * j + r == TILES - 1
            h0 = tile_of(j, r) * ROWS + (1 if r % 2 == 0 or last else 0)
            whole = [(rows(dram, h0, ROWS - last), tile[:, 1:] if last else tile, done)]
            if last:
                whole.append((rows(dram, 0, 1), tile[:, 0:1], row0))
            for far, near, signal in whole:
                sp.dma_start(far if store else near, near if store else far).then_inc(signal, 16)

        block = ctx.enter_context(nc.Block())

        def inverse_std(dve, chain, m2, v, y, t):
            chain.add(dve.tensor_scalar(v, m2, -0.5 / C, -0.5 * LN_EPS, ALU.mult, ALU.add))
            chain.settle()
            chain.add(dve.tensor_scalar(y.bitcast(I32), v.bitcast(I32), -0.5, MAGIC, ALU.mult, ALU.add))
            for _ in range(3):
                chain.settle()
                chain.add(dve.tensor_tensor(t, y, y, ALU.mult))
                chain.settle()
                chain.add(dve.tensor_tensor(t, t, v, ALU.mult))
                chain.settle()
                chain.add(dve.scalar_tensor_tensor(y, t, 1.5, y, ALU.add, ALU.mult))
            chain.settle()

        def place(c):
            return c % HALF, c // HALF

        def evict_a(copy, q, cg, r):
            dst = spec[:, :, :, bass.ds(GROUP * cg, GROUP), q].rearrange("p k r c -> p (k r) c")
            return copy(dst, ps[:, 2 + r].rearrange("p (i k) -> p k i", i=GROUP))

        def evict_v(copy, cg, r):
            return copy(zbuf[:, :, bass.ds(GROUP * cg, GROUP)], ps[:, r].rearrange("p (i h) -> p h i", i=GROUP))

        @block.sync
        def _(sp):
            def load_spectral(layer):
                p = params[layer]
                sp.dma_start(wraw[:, :, :, :, :], p["blocks"]).then_inc(spec_in, 16)
                sp.dma_start(vectors[:, 0:3, :], p["vectors"]).then_inc(spec_in, 16)
                sp.dma_start(b2rep[:, :, :, :], p["b2"].unsqueeze(0).to_broadcast([P, 2, 2, HALF])).then_inc(spec_in, 16)
                sp.dma_start(betarow[0:1, :], p["n1_b"]).then_inc(spec_in, 16)

            def load_gain(layer):
                sp.dma_start(gain1[:, :], params[layer]["n1_g"].to_broadcast([P, C])).then_inc(gain_in, 16)

            def load_raw(layer):
                sp.dma_start(mw1raw[:, :], params[layer]["mw1"]).then_inc(raw_in, 16)
                sp.dma_start(columns[:, :], params[layer]["columns"]).then_inc(raw_in, 16)

            def load_mlp(layer):
                p = params[layer]
                sp.dma_start(mw2[:, :, :], p["mw2"].rearrange("(m k) c -> k m c", m=CHUNKS)).then_inc(mlp_in, 16)
                sp.dma_start(mb2rep[:, :], p["mb2"].to_broadcast([P, C])).then_inc(mlp_in, 16)

            n = PB * ROWS
            load_spectral(0)
            sp.dma_start(resid[:, 0:n, :], rows(source[0], 1, n)).then_inc(x_in[0], 16)
            load_gain(0)
            sp.dma_start(resid[:, n:2 * n, :], rows(source[0], n + 1, n)).then_inc(x_in[1], 16)
            sp.dma_start(resid[:, HALF, :], source[0][0]).then_inc(row0_in, 16)
            sp.dma_start(resid[:, HALF + 1:3 * n, :], rows(source[0], HALF + 1, n - 1)).then_inc(x_in[2], 16)
            sp.dma_start(resid[:, 3 * n:, :], rows(source[0], 3 * n, n)).then_inc(x_in[3], 16)

            for s, (layer, _) in enumerate(STEPS):
                last = s == len(STEPS) - 1
                sp.wait_ge(r_done, TILES * (s + 1))
                if s:
                    for i in range(2):
                        sp.wait_ge(x_st[i], 16 * (TILES // 2) * s)
                    sp.wait_ge(row0_st, 16 * s)
                load_raw(layer)
                sp.wait_ge(ih_mm, CGROUPS * (s + 1))
                load_mlp(layer)
                if not last and STEPS[s + 1][0] != layer:
                    load_gain(layer + 1)
                    load_spectral(layer + 1)

                def load(j, r):
                    sp.wait_ge(r_done, TILES * (s + 1) + 4 * j + r - 3)
                    transfers(sp, source[s + 1], xnext[:, r], j, r, xn_in[r], row0_in, False)

                def store(j, r):
                    sp.wait_ge(x_out, TILES * s + 4 * j + r + 1)
                    transfers(sp, target[s], xout[:, r % 2], j, r, x_st[r % 2], row0_st, True)

                if not last:
                    for r in range(4):
                        load(0, r)
                    with sp.Fori(1, TILES // 4 - 1) as j:
                        for r in range(4):
                            store(j - 1, r)
                            load(j, r)
                    for r in range(4):
                        store(TILES // 4 - 2, r)
                        load(TILES // 4 - 1, r)
                else:
                    with sp.Fori(0, TILES // 4 - 1) as j:
                        for r in range(4):
                            store(j, r)
                for r in range(4):
                    store(TILES // 4 - 1, r)
            for i in range(2):
                sp.wait_ge(x_st[i], 16 * (TILES // 2) * len(STEPS))
            sp.wait_ge(row0_st, 16 * len(STEPS))

        @block.tensor
        def _(pe):
            def dc_bias(n):
                pe.wait_ge(spec_built, n + 1)
                if n:
                    pe.wait_ge(y_out, Y_CREDIT + TILES * IMAGES * n)
                for q in range(2):
                    mm = pe.matmul(ps[:, 7, q:q + 1], w1s[0:HALF, 0, q].rearrange("p r c -> p (r c)"),
                                   beta64[0:HALF, q:q + 1], start=(q == 0), stop=True, skip_group_check=True)
                mm.then_inc(dc_mm, 1)

            def dft_w(s):
                pe.wait_ge(z_dve, Z_DVE0 + TILES * s)
                pe.wait_ge(z_act, PRO_ACT * (TILES // PB))
                for cg in range(CGROUPS):
                    if cg >= 4:
                        pe.wait_ge(a_dve if cg % 2 else a_act, CGROUPS // 2 * s + (cg - 4) // 2 + 1)
                    for i in range(GROUP):
                        mm = pe.matmul(ps[:, 2 + cg % 4, P * i:P * i + P], zbuf[:, :, GROUP * cg + i], FW,
                                       start=True, stop=True)
                    mm.then_inc(s1_mm, 1)

            def dft_h(s, n):
                b, q = n // 2, n % 2
                if n >= 2:
                    pe.wait_ge(g_out, 2 * BATCHES * s + n - 1)
                for i in range(GROUP):
                    mm = pe.matmul(ps[:, q, P * i:P * i + P],
                                   spec[:, GROUP * b + i, :, :, q].rearrange("p r c -> p (r c)"), FH,
                                   start=True, stop=True)
                mm.then_inc(s2_mm, 1)

            def mix1(s, n):
                b, q = n // 2, n % 2
                if b < BATCHES:
                    pe.wait_ge(g_out, 2 * BATCHES * s + n + 1)
                if n >= 2:
                    pe.wait_ge(u_out, UNITS * s + n - 1)

                def both(dst, src, w_even, w_odd, start):
                    pe.matmul(dst[:, 0:EVEN], w_even, src[:, 0:EVEN], start=start, stop=True, skip_group_check=True)
                    return pe.matmul(dst[:, EVEN:], w_odd, src[:, EVEN:], start=False, stop=True,
                                     skip_group_check=True)

                even, odd = (w1s[:, i, q].rearrange("p r c -> p (r c)") for i in range(2))
                if b == BATCHES:
                    dst = ps[:, 2 + q, 0:P].rearrange("p (k j) -> p k j", j=1)
                    mm = both(dst, nyq[HALF:P, q].rearrange("p (k j) -> p k j", j=1), odd[HALF:P], even[HALF:P], True)
                else:
                    dst = ps[:, 2 + q].rearrange("p (k j) -> p k j", j=GROUP)
                    src = gsb[:, q]
                    if b:
                        mm = both(dst, src, even, odd, True)
                    else:
                        both(dst[:, :, 1:], src[:, :, 1:], even, odd, True)
                        both(dst[:, :, 0:1], src[0:HALF, :, 0:1], even[0:HALF], odd[0:HALF], False)
                        mm = pe.matmul(ps[:, 2 + q, 0:1], IDENT, dcbias[:, q:q + 1], start=False, stop=True,
                                       skip_group_check=True)
                mm.then_inc(m1_mm, 1)

            def mix2(s, n):
                b, q = n // 2, n % 2
                kws = GROUP if b < BATCHES else 1
                pe.wait_ge(o_out, UNITS * s + n + 1)
                if n >= 2:
                    pe.wait_ge(v_out, UNITS * s + n - 1)
                src = osb[:, q].rearrange("p k j -> p (k j)")
                for i in range(kws):
                    mm = pe.matmul(ps[:, 4 + q, P * i:P * i + P], src[:, i:i + (P - 1) * kws + 1:kws],
                                   w2s[:, q].rearrange("p r c -> p (r c)"), start=True, stop=True)
                mm.then_inc(m2_mm, 1)

            def filter_(s):
                pe.wait_ge(a_act, CGROUPS // 2 * (s + 1))
                pe.wait_ge(a_dve, CGROUPS // 2 * (s + 1))
                pe.wait_ge(y_out, Y_CREDIT + TILES * s)
                pe.wait_ge(spec_done, 1 + s // IMAGES)
                dft_h(s, 0)
                dft_h(s, 1)
                mix1(s, 0)
                for n in range(UNITS):
                    if n + 2 < 2 * BATCHES:
                        dft_h(s, n + 2)
                    if n + 1 < UNITS:
                        mix1(s, n + 1)
                    mix2(s, n)

            def idft_h(s):
                pe.wait_ge(t_edge, s + 1)
                for i, m in enumerate((REVERSE, IDENT)):
                    mm = pe.matmul(ps[:, 6, 0:2 * C], m, tedge[:, i].rearrange("p k c -> p (k c)"),
                                   start=(i == 0), stop=(i == 1))
                mm.then_inc(x_mm, 1)
                pe.wait_ge(y_done, (UNITS + 1) * (s + 1))
                for cg in range(CGROUPS):
                    if cg >= 4:
                        pe.wait_ge(v_dve if cg % 2 else v_act, CGROUPS // 2 * s + (cg - 4) // 2 + 1)
                    for i in range(GROUP):
                        ch, q = place(GROUP * cg + i)
                        mm = pe.matmul(ps[:, cg % 4, P * i:P * i + P],
                                       spec[:, :, :, ch, q].rearrange("p k r -> p (k r)"), IH, start=True, stop=True)
                    mm.then_inc(ih_mm, 1)

            def mlp_bias(s):
                pe.wait_ge(raw_in, RAW_IN * (s + 1))
                for m in range(CHUNKS):
                    mm = pe.matmul(ps[:, 3, m:m + 1], mw1raw[:, P * m:P * m + P], beta2[:, 0:1],
                                   start=(m == 0), stop=(m == CHUNKS - 1), skip_group_check=True)
                mm.then_inc(mlp_b_mm, 1)

            def idft_w(s, p):
                pe.wait_ge(h2_done, TILES * s + 2 * p)
                even = zbuf[:, bass.ds(p * ROWS, ROWS), :]
                odd = zbuf[:, bass.ds(p * -ROWS + (H - ROWS), ROWS), :]
                pe.matmul(ps[:, 6], DE, even, start=True, stop=True)
                if isinstance(p, int) and p == PAIRS - 1:
                    pe.matmul(ps[:, 7, C:], DO, odd[:, 1:], start=True, stop=True, skip_group_check=True)
                    mm = pe.matmul(ps[:, 7, 0:C], DE, odd[:, 0], start=False, stop=True, skip_group_check=True)
                else:
                    mm = pe.matmul(ps[:, 7], DO, odd, start=True, stop=True)
                mm.then_inc(iw_mm, 1)

            def turn(s, n, r):
                pe.wait_ge(hn_done, TILES * s + n + 1)
                if not (isinstance(n, int) and n < 2):
                    pe.wait_ge(lo_out, TILES * s + n - 1)
                for i in range(ROWS):
                    mm = pe.transpose(ps[:, 4 + r % 2, P * i:P * i + P], hn[:, r % 2, i, :], IDENT)
                mm.then_inc(t_mm, 1)

            def fc1(s, n, r, m):
                if m == 0:
                    pe.wait_ge(lo_out, TILES * s + n + 1)
                if not (isinstance(n, int) and n == 0 and m < 2):
                    pe.wait_ge(gelu_out, CHUNKS * TILES * s + CHUNKS * n + m - 1)
                h, l = mw1h[:, P * m:P * m + P], mw1l[:, P * m:P * m + P]
                bank = ps[:, 2 + m % 2]
                pe.matmul(bank, h, hth[:, r % 2, :], start=True, stop=False)
                pe.matmul(bank, h, htl[:, r % 2, :], start=False, stop=False)
                pe.matmul(bank, l, hth[:, r % 2, :], start=False, stop=True).then_inc(f1_mm, 1)

            def fc2(s, n, r, m):
                pe.wait_ge(gelu_out, CHUNKS * TILES * s + CHUNKS * n + m + 1)
                if m == 0:
                    pe.wait_ge(y_out, Y_CREDIT + TILES * s + n - 1)
                for i in range(ROWS):
                    mm = pe.matmul(ps[:, r % 2, P * i:P * i + P], gel[:, r % 2, m, P * i:P * i + P], mw2[:, m, :],
                                   start=(m == 0 and i == 0), stop=(m == CHUNKS - 1), skip_group_check=True)
                if m == CHUNKS - 1:
                    mm.then_inc(f2_mm, 1)

            def mlp(s):
                pe.wait_ge(v_act, CGROUPS // 2 * (s + 1))
                pe.wait_ge(v_dve, CGROUPS // 2 * (s + 1))
                idft_w(s, 0)
                mlp_bias(s)
                idft_w(s, 1)
                turn(s, 0, 0)
                turn(s, 1, 1)
                pe.wait_ge(mlp_b, s + 1)
                pe.wait_ge(mlp_w, s + 1)
                for m in range(CHUNKS):
                    fc1(s, 0, 0, m)
                pe.wait_ge(mlp_in, MLP_IN * (s + 1))

                def tile(j, r):
                    n = 4 * j + r
                    known = n if isinstance(j, int) else 4
                    for m in range(CHUNKS):
                        if known + 1 < TILES:
                            fc1(s, n + 1, r + 1, m)
                        fc2(s, n, r, m)
                        if m == 0 and r % 2 == 0 and known + 4 < TILES:
                            idft_w(s, 2 * j + r // 2 + 2)
                        if m == 1 and known + 2 < TILES:
                            turn(s, n + 2, r + 2)

                with pe.Fori(0, TILES // 4 - 2) as j:
                    for r in range(4):
                        tile(j, r)
                for n in range(TILES - 8, TILES):
                    tile(n // 4, n % 4)

            pe.wait_ge(cst_in, 16)
            for s in range(len(STEPS)):
                if s % IMAGES == 0:
                    dc_bias(s // IMAGES)
                dft_w(s)
                filter_(s)
                idft_h(s)
                mlp(s)

        @block.scalar
        def _(act):
            def a_out(s, q, j, r):
                act.wait_ge(s1_mm, CGROUPS * s + CGROUPS // 2 * q + 4 * j + r + 1)
                evict_a(act.copy, q, 4 * j + r, r).then_inc(a_act, 1)

            def g_copy(s, n, q, first=False):
                act.wait_ge(s2_mm, 2 * BATCHES * s + n + 1)
                if first:
                    act.copy(nyq[HALF:P, q], ps[HALF:P, q, 0:P])
                else:
                    act.wait_ge(m1_mm, UNITS * s + n - 1)
                src = ps[:, q].rearrange("p (j k) -> p k j", j=GROUP)
                act.copy(gsb[:, q], src).then_inc(g_out, 1)

            def e_copy(s, n, q, kws=GROUP):
                act.wait_ge(m1_mm, UNITS * s + n + 1)
                dst = usb[:, q].rearrange("p k j -> p (k j)")[:, 0:EVEN * kws]
                act.copy(dst, ps[:, 2 + q, 0:EVEN * kws]).then_inc(e_out, 1)

            def o_relu(s, n, q, kws=GROUP, first=False):
                act.wait_ge(u_out, UNITS * s + n + 1)
                if not first:
                    act.wait_ge(m2_mm, UNITS * s + n - 1)
                dst = osb[:, q].rearrange("p k j -> p (k j)")[:, 0:P * kws]
                src = usb[:, q].rearrange("p k j -> p (k j)")[:, 0:P * kws]
                act.activation(dst, src, ACT.Relu, bias=b1v[:, q:q + 1]).then_inc(o_out, 1)

            def v_out_(s, cg, r):
                act.wait_ge(ih_mm, CGROUPS * s + cg + 1)
                evict_v(act.copy, cg, r).then_inc(v_act, 1)

            def normal(s, j, r, part):
                n = 4 * j + r
                if part == 0:
                    act.wait_ge(rs_done, PAIRS * s + 2 * j + r // 2 + 1)
                    if not (isinstance(j, int) and n < 2):
                        act.wait_ge(t_mm, TILES * s + n - 1)
                for i in (2 * part, 2 * part + 1):
                    row = resid[:, bass.ds(ROWS * tile_of(j, r) + i, 1), :].rearrange("p h c -> p (h c)")
                    ins = act.activation(hn[:, r % 2, i, :], row, ACT.Identity,
                                         bias=shift[:, r // 2, r % 2 * ROWS + i:r % 2 * ROWS + i + 1],
                                         scale=rstd[:, r // 2, r % 2 * ROWS + i:r % 2 * ROWS + i + 1])
                if part:
                    ins.then_inc(hn_done, 1)

            def hi(s, n, r):
                act.wait_ge(t_mm, TILES * s + n + 1)
                act.copy(hth[:, r % 2, :], ps[:, 4 + r % 2]).then_inc(hi_out, 1)

            def y_copy(s, n, r):
                act.wait_ge(f2_mm, TILES * s + n + 1)
                if not (isinstance(n, int) and s == 0 and n < 2):
                    act.wait_ge(x_st[r % 2], 16 * (TILES // 2 * s) + (n - r % 2) * 8)
                if isinstance(n, int) and n == 1:
                    act.wait_ge(mlp_w, s + 1)
                    if s:
                        act.wait_ge(row0_st, 16 * s)
                act.copy(xout[:, r % 2].rearrange("p h c -> p (h c)"), ps[:, r % 2]).then_inc(y_out, 1)

            def gelu(s, n, r, m):
                act.wait_ge(f1_mm, CHUNKS * TILES * s + CHUNKS * n + m + 1)
                if m == 0 and not (isinstance(n, int) and n < 2):
                    act.wait_ge(f2_mm, TILES * s + n - 1)
                act.activation(gel[:, r % 2, m, :], ps[:, 2 + m % 2], ACT.Gelu, bias=mb1f[:, m:m + 1]).then_inc(
                    gelu_out, 1)

            act.dma_start(cst[:, CONSTS - 2 * BLOCKS:], consts[:, CONSTS - 2 * BLOCKS:]).then_inc(mask_in, 16)
            act.dma_start(cst[:, :CONSTS - 2 * BLOCKS], consts[:, :CONSTS - 2 * BLOCKS]).then_inc(cst_in, 16)
            for b in range(TILES // PB):
                act.wait_ge(st_pro, b + 1)
                for t in range(PB - PRO_ACT, PB):
                    for i in range(ROWS):
                        h = (PB * b + t) * ROWS + i
                        ins = act.activation(zbuf[:, h, :], resid[:, h, :], ACT.Identity,
                                             bias=pnm[:, h:h + 1], scale=prs[:, h:h + 1])
                    ins.then_inc(z_act, 1)
            for s in range(len(STEPS)):
                if s:
                    act.wait_ge(r_done, TILES * (s + 1))
                for q in range(2):
                    with act.Fori(0, CGROUPS // 8) as j:
                        for r in (0, 2):
                            a_out(s, q, j, r)
                act.wait_ge(r_done, TILES * (s + 1))
                g_copy(s, 0, 0, first=True)

                def batch(b, first=False, last=False):
                    g_copy(s, 2 * b + 1, 1, first=first)
                    e_copy(s, 2 * b, 0)
                    o_relu(s, 2 * b, 0, first=first)
                    if not last:
                        g_copy(s, 2 * b + 2, 0)
                    e_copy(s, 2 * b + 1, 1)
                    o_relu(s, 2 * b + 1, 1, first=first)

                batch(0, first=True)
                with act.Fori(1, BATCHES - 1) as b:
                    batch(b)
                batch(BATCHES - 1, last=True)
                for q in range(2):
                    e_copy(s, UNITS - 2 + q, q, kws=1)
                    o_relu(s, UNITS - 2 + q, q, kws=1)
                with act.Fori(0, CGROUPS // 4) as j:
                    for r in (0, 2):
                        v_out_(s, 4 * j + r, r)
                for n in range(2):
                    for part in range(2):
                        normal(s, 0, n, part)
                    hi(s, n, n)
                act.wait_ge(mlp_b, s + 1)
                for m in range(CHUNKS):
                    gelu(s, 0, 0, m)

                def tile(j, r):
                    n = 4 * j + r
                    known = n if isinstance(j, int) else 4
                    for m in range(CHUNKS):
                        if m == 1 and known:
                            y_copy(s, n - 1, (r - 1) % 4)
                        if m == 2 and known + 2 < TILES:
                            hi(s, n + 2, (r + 2) % 4)
                        if known + 1 < TILES:
                            gelu(s, n + 1, (r + 1) % 4, m)
                        if m == 0 and known + 2 < TILES:
                            normal(s, j + (r + 2) // 4, (r + 2) % 4, 1)
                        if m == 3 and known + 3 < TILES:
                            normal(s, j + (r + 3) // 4, (r + 3) % 4, 0)

                normal(s, 0, 2, 0)
                for r in range(4):
                    tile(0, r)
                with act.Fori(1, TILES // 4 - 1) as j:
                    for r in range(4):
                        tile(j, r)
                for r in range(4):
                    tile(TILES // 4 - 1, r)
                y_copy(s, TILES - 1, 3)

        @block.vector
        def _(dve):
            own = Chain(dve, dve_own)

            def build_spectral(n):
                dve.wait_ge(spec_in, SPEC_IN * (n + 1))
                if n:
                    dve.wait_ge(ih_mm, CGROUPS * n * IMAGES)
                re, im = slice(0, HALF), slice(HALF, P)
                jobs = [(w1s[:, 0], wraw[:, 0], [(re, 0, 0, 0), (re, 1, 1, 0), (im, 0, 1, 1), (im, 1, 0, 0)]),
                        (w1s[:, 1], wraw[:, 0], [(re, 0, 1, 0), (re, 1, 0, 1), (im, 0, 0, 0), (im, 1, 1, 0)]),
                        (w2s[:, :], wraw[:, 1], [(re, 0, 0, 0), (re, 1, 1, 0), (im, 0, 1, 1), (im, 1, 0, 0)])]
                for dst, raw, parts in jobs:
                    for part, col, j, sign in parts:
                        for q in range(2):
                            src = raw[part, j, q, :].unsqueeze(1).to_broadcast([HALF, BLOCKS, BLOCK])
                            m = mask[part, sign, :].unsqueeze(2).to_broadcast([HALF, BLOCKS, BLOCK])
                            to = dst[part, q, col, :].rearrange("p (b o) -> p b o", b=BLOCKS)
                            own.add(dve.tensor_tensor(to, src, m, ALU.mult))
                own.settle()
                dve.nop().then_inc(spec_built, 1)
                dve.wait_ge(dc_mm, n + 1)
                own.add(dve.tensor_scalar(dcbias[:, :], ps[:, 7, 0:2], DC, None, ALU.mult))
                own.add(dve.tensor_scalar(betarow[0:1, :], betarow[0:1, :], DC, None, ALU.mult))
                for q in range(2):
                    for kind in range(2):
                        t = w1s[:, kind, q].rearrange("p r c -> p (r c)")
                        own.add(dve.tensor_scalar(t, t, gain64[:, q:q + 1], None, ALU.mult))
                own.settle()
                dve.nop().then_inc(spec_done, 1)

            def bn(buf, row, to):
                for i in range(ROWS - 2, -1, -2):
                    src = buf[:, bass.ds(row + i, 2), :].rearrange("p h c -> p c h")
                    ins = dve.bn_stats(to[:, i:i + 2, :].rearrange("p h k -> p (h k)"), src)
                return ins

            dve.wait_ge(mask_in, 16)
            dve.nop().then_inc(y_out, Y_CREDIT)
            build_spectral(0)
            for b in range(TILES // PB):
                dve.wait_ge(x_in[b], 16)
                if b == TILES // PB // 2:
                    dve.wait_ge(row0_in, 16)
                h0 = PB * ROWS * b
                own_rows = slice(h0, h0 + PB * ROWS)
                for t in range(PB):
                    h = h0 + ROWS * t
                    own.add(bn(resid, h, pst[:, h:h + ROWS, :]))
                own.settle()
                inverse_std(dve, own, pst[:, own_rows, 2], pva[:, :], prs[:, own_rows], pn0[:, :])
                own.add(dve.scalar_tensor_tensor(pnm[:, own_rows], pst[:, own_rows, 1], -1.0, prs[:, own_rows],
                                                 ALU.mult, ALU.mult))
                own.settle()
                dve.nop().then_inc(st_pro, 1)
                for t in range(PB - PRO_ACT):
                    for i in range(ROWS):
                        h = h0 + ROWS * t + i
                        ins = dve.tensor_scalar(zbuf[:, h, :], resid[:, h, :], pst[:, h, 1:2], prs[:, h:h + 1],
                                                ALU.subtract, ALU.mult)
                    ins.then_inc(z_dve, 1)

            def a_out(s, q, j, r):
                dve.wait_ge(s1_mm, CGROUPS * s + CGROUPS // 2 * q + 4 * j + r + 1)
                evict_a(dve.tensor_copy, q, 4 * j + r, r).then_inc(a_dve, 1)

            def combine(s, n, q, kws=GROUP):
                dve.wait_ge(e_out, UNITS * s + n + 1)
                odd = ps[:, 2 + q, EVEN * kws:P * kws].rearrange("p (k j) -> p k j", j=kws)
                u = usb[:, q].rearrange("p k j -> p (k j)")[:, 0:P * kws].rearrange("p (k j) -> p k j", j=kws)
                ops = (ALU.add, ALU.subtract) if kws > 1 else (ALU.subtract, ALU.add)
                dve.tensor_tensor(u[:, EVEN:], u[:, 1:KWS], odd, ops[1])
                ins = dve.tensor_tensor(u[:, 1:KWS], u[:, 1:KWS], odd, ops[0])
                ins.then_inc(u_out, 1)

            def shrink(s, n, b, q, kws=GROUP):
                dve.wait_ge(m2_mm, UNITS * s + n + 1)
                bias = b2rep[:, q].rearrange("p r c -> p (r c)").unsqueeze(1).to_broadcast([P, kws, P])
                v = vsb[:, q].rearrange("p j r c -> p j (r c)")[:, 0:kws]
                cl = csb[:, q].rearrange("p j r c -> p j (r c)")[:, 0:kws]
                src = ps[:, 4 + q, 0:P * kws].rearrange("p (j k) -> p j k", j=kws)
                dve.tensor_tensor(v, src, bias, ALU.add).then_inc(v_out, 1)
                dve.wait_ge(v_out, UNITS * s + n + 1)
                own.add(dve.tensor_scalar(cl, v, -LAM, LAM, ALU.max, ALU.min))
                own.settle()
                v, cl = vsb[:, q], csb[:, q]
                if kws == 1 or isinstance(b, int) and b == 0:
                    edge = yedge[:, 0 if kws > 1 else 1, :, :, q]
                    ins = dve.tensor_tensor(edge, v[:, 0], cl[:, 0], ALU.subtract)
                    if kws == 1:
                        ins.then_inc(y_done, 1)
                        return
                    own.add(ins)
                    dst, v, cl = spec[:, 1:GROUP, :, :, q], v[:, 1:], cl[:, 1:]
                else:
                    dst = spec[:, bass.ds(GROUP * b, GROUP), :, :, q]
                dve.tensor_tensor(dst, v, cl, ALU.subtract).then_inc(y_done, 1)

            def edges(s):
                dve.wait_ge(y_done, (UNITS + 1) * s + UNITS)
                own.settle()
                dve.wait_ge(spec_done, 1 + s // IMAGES)
                shift = yedge[0:1, 0, 0].rearrange("p c q -> p q c")
                own.add(dve.tensor_tensor(shift, shift, betarow[0:1, :].rearrange("p (q c) -> p q c", q=2), ALU.add))
                own.settle()
                for i, op in enumerate((ALU.add, ALU.subtract)):
                    ins = dve.tensor_tensor(tedge[:, i], yedge[:, :, 0].rearrange("p k c q -> p k (c q)"),
                                            yedge[:, :, 1].rearrange("p k c q -> p k (c q)"), op)
                ins.then_inc(t_edge, 1)
                dve.wait_ge(x_mm, s + 1)
                dve.tensor_scalar(spec[:, 0].rearrange("p r c q -> p (r c q)"), ps[:, 6, 0:2 * C], 0.5, None,
                                  ALU.mult).then_inc(y_done, 1)

            def v_out_(s, cg, r):
                dve.wait_ge(ih_mm, CGROUPS * s + cg + 1)
                evict_v(dve.tensor_copy, cg, r).then_inc(v_dve, 1)

            def split_weights(s):
                dve.wait_ge(raw_in, RAW_IN * (s + 1))
                own.add(dve.tensor_scalar(mw1h[:, :], mw1raw[:, :], gain2[:, 0:1], None, ALU.mult))
                own.settle()
                dve.scalar_tensor_tensor(mw1l[:, :], mw1raw[:, :], gain2[:, 0:1], mw1h[:, :].bitcast(F32),
                                         ALU.mult, ALU.subtract).then_inc(mlp_w, 1)
                dve.wait_ge(mlp_b_mm, s + 1)
                dve.tensor_tensor(mb1f[:, :], ps[:, 3, 0:CHUNKS], mb1[:, :], ALU.add).then_inc(mlp_b, 1)

            def rows_of(buf, j, r, n=ROWS, i=0):
                return buf[:, bass.ds(ROWS * tile_of(j, r) + i, n), :].rearrange("p h c -> p (h c)")

            def h2(s, i, h):
                dve.wait_ge(iw_mm, PAIRS * s + 2 * i + h + 1)
                last = isinstance(i, int) and 2 * i + h == PAIRS - 1
                top, low = (resid[:, bass.ds(ROWS * tile_of(i, 2 * h + e), ROWS), :] for e in range(2))
                even = ps[:, 6].rearrange("p (h c) -> p h c", h=ROWS)
                odd = ps[:, 7].rearrange("p (h c) -> p h c", h=ROWS)
                own.add(dve.tensor_tensor(top, even, top, ALU.add))
                if last:
                    dve.tensor_tensor(low[:, 0:1], odd[:, 0:1], low[:, 0:1], ALU.add)
                    own.add(dve.tensor_tensor(low[:, 1:], even[:, 2::-1], low[:, 1:], ALU.add))
                    own.settle()
                    dve.tensor_tensor(top[:, 0:3], odd[:, :0:-1], top[:, 0:3], ALU.add)
                    ins = dve.tensor_tensor(low[:, 1:], low[:, 1:], odd[:, 1:], ALU.subtract)
                else:
                    own.add(dve.tensor_tensor(low, even[:, ::-1], low, ALU.add))
                    own.settle()
                    dve.tensor_tensor(top, odd[:, ::-1], top, ALU.add)
                    ins = dve.tensor_tensor(low, low, odd, ALU.subtract)
                ins.then_inc(h2_done, 2)

            def lower(s, n, r):
                dve.wait_ge(hi_out, TILES * s + n + 1)
                dve.tensor_tensor(htl[:, r % 2, :], ps[:, 4 + r % 2], hth[:, r % 2, :].bitcast(F32),
                                  ALU.subtract).then_inc(lo_out, 1)

            def z_new(i, h, e):
                for k in range(ROWS):
                    row = 2 * ROWS + e * ROWS + k
                    ins = dve.tensor_scalar(rows_of(zbuf, i, 2 * h + e, 1, k), xnext[:, 2 * h + e, k, :],
                                            stats[:, h, row, 1:2], rstd[:, h, row:row + 1],
                                            ALU.subtract, ALU.mult)
                ins.then_inc(z_dve, 1)

            for s in range(len(STEPS)):
                last = s == len(STEPS) - 1
                if s:
                    dve.wait_ge(r_done, TILES * (s + 1))
                for q in range(2):
                    with dve.Fori(0, CGROUPS // 8) as j:
                        for r in (1, 3):
                            a_out(s, q, j, r)
                combine(s, 0, 0)
                for q in range(2):
                    combine(s, q + 1, 1 - q)
                    shrink(s, q, 0, q)
                with dve.Fori(1, BATCHES - 1) as b:
                    own.enter(b, 2, 1)
                    for q in range(2):
                        combine(s, 2 * b + q + 1, 1 - q)
                        shrink(s, 2 * b + q, b, q)
                own.leave(BATCHES - 1)
                for q in range(2):
                    combine(s, UNITS - 3 + q, 1 - q, kws=1 if q else GROUP)
                    shrink(s, UNITS - 4 + q, BATCHES - 1, q)
                combine(s, UNITS - 1, 1, kws=1)
                for q in range(2):
                    shrink(s, UNITS - 2 + q, BATCHES, q, kws=1)
                edges(s)
                with dve.Fori(0, CGROUPS // 4) as j:
                    for r in (1, 3):
                        v_out_(s, 4 * j + r, r)

                def pair(i, h):
                    q = 2 * i + h
                    known = q if isinstance(i, int) else 4
                    main = known < PAIRS
                    nxt = not last and known >= LAG
                    if main:
                        if known >= 2:
                            dve.wait_ge(hn_done, TILES * s + 2 * q - 2)
                        h2(s, i, h)
                    if 1 <= known <= PAIRS:
                        lower(s, 2 * q - 2, (2 * h - 2) % 4)
                    if main:
                        dve.wait_ge(h2_done, TILES * s + 2 * q + 2)
                        for e in range(2):
                            ins = bn(resid, tile_of(i, 2 * h + e) * ROWS, stats[:, h, e * ROWS:(e + 1) * ROWS, :])
                    if nxt:
                        for e in range(2):
                            dve.wait_ge(xn_in[2 * h + e], 16 * (TILES // 4 * s + i))
                            if isinstance(i, int) and 2 * (q - LAG) + e == TILES - 1:
                                dve.wait_ge(row0_in, 16 * (s + 2))
                            rows_ = slice((2 + e) * ROWS, (3 + e) * ROWS)
                            ins = bn(xnext[:, 2 * h + e], 0, stats[:, h, rows_, :])
                    if main or nxt:
                        own.add(ins)
                        own.settle()
                        a, b = 0 if main else 2 * ROWS, 4 * ROWS if nxt else 2 * ROWS
                        inverse_std(dve, own, stats[:, h, a:b, 2], var[:, a:b], rstd[:, h, a:b], nt0[:, a:b])
                    if main:
                        dve.scalar_tensor_tensor(shift[:, h], stats[:, h, 0:2 * ROWS, 1], -1.0, rstd[:, h, 0:2 * ROWS],
                                                 ALU.mult, ALU.mult).then_inc(rs_done, 1)
                    if nxt:
                        z_new(i - 1, h, 0)
                        z_new(i - 1, h, 1)
                    if 1 <= known <= PAIRS:
                        lower(s, 2 * q - 1, (2 * h - 1) % 4)

                pair(0, 0)
                split_weights(s)
                pair(0, 1)
                with dve.Fori(1, PAIRS // 2 - 1) as i:
                    own.enter(i, 2 * 14, 1)
                    for h in range(2):
                        pair(i, h)
                own.leave(PAIRS // 2 - 1)
                for q in range(PAIRS - 2, PAIRS + LAG):
                    pair(q // 2, q % 2)
                if s + 1 < len(STEPS) and STEPS[s + 1][0] != STEPS[s][0]:
                    build_spectral(STEPS[s + 1][0])

        @block.gpsimd
        def _(pool):

            def scale(h0, tmp):
                z = zbuf[:, h0, :]
                g = gain1[:, :].unsqueeze(1).to_broadcast([P, ROWS, C])
                pool.tensor_tensor(tmp, z, g, ALU.mult).then_inc(gz_done, 1)

            def residual(h0, xtile, tmp):
                pool.tensor_tensor(resid[:, h0, :], xtile, tmp, ALU.add).then_inc(r_done, 1)

            pool.wait_ge(gain_in, 16)
            done = [0, 0]
            for t in range(TILES):
                who = 0 if t % PB < PB - PRO_ACT else 1
                done[who] += 1
                pool.wait_ge((z_dve, z_act)[who], done[who])
                if t >= 2:
                    pool.wait_ge(r_done, t - 1)
                h = slice(ROWS * t, ROWS * t + ROWS)
                scale(h, xout[:, t % 2])
                pool.wait_ge(gz_done, t + 1)
                residual(h, resid[:, h, :], xout[:, t % 2])

            for s in range(len(STEPS)):
                last = s == len(STEPS) - 1
                if not last and STEPS[s + 1][0] != STEPS[s][0]:
                    pool.wait_ge(gain_in, 16 * 2)

                pool.wait_ge(mlp_in, MLP_IN * (s + 1))

                def x_new(s, j, r):
                    n = 4 * j + r
                    pool.wait_ge(y_out, Y_CREDIT + TILES * s + n + 1)
                    pool.wait_ge(mb2_done, TILES * s + n + 1)
                    first = 2 * ROWS * j + r // 2 * ROWS
                    if r % 2:
                        first = first * -1 + (H - ROWS)
                    t = resid[:, bass.ds(first, ROWS), :].rearrange("p h c -> p (h c)")
                    y = xout[:, r % 2].rearrange("p h c -> p (h c)")
                    pool.tensor_tensor(y, y, t, ALU.add).then_inc(x_out, 1)

                def bias(s, j, r):
                    t = resid[:, bass.ds(ROWS * tile_of(j, r), ROWS), :]
                    b = mb2rep[:, :].unsqueeze(1).to_broadcast([P, ROWS, C])
                    pool.tensor_tensor(t, t, b, ALU.add).then_inc(mb2_done, 1)

                def tile(j, r):
                    n = 4 * j + r
                    known = n if isinstance(j, int) else 8
                    nxt = not last
                    main = known < TILES
                    m = n - 4
                    again = nxt and known >= 4
                    if again:
                        h0 = bass.ds(ROWS * tile_of(j - 1, r), ROWS)
                        pool.wait_ge(z_dve, Z_DVE0 + TILES * s + m + 1)
                        pool.wait_ge(r_done, TILES * (s + 1) + m - 1)
                        scale(h0, gz[:, r % 2])
                    if 4 <= known < TILES + 4:
                        x_new(s, j - 1, r)
                    if again:
                        pool.wait_ge(gz_done, TILES * (s + 1) + m + 1)
                        pool.wait_ge(x_out, TILES * s + m + 1)
                    if 2 <= known <= TILES + 1:
                        pool.wait_ge(hn_done, TILES * s + n - 1)
                        bias(s, j + (r - 2) // 4, (r - 2) % 4)
                    if again:
                        residual(h0, xnext[:, r], gz[:, r % 2])

                for n in range(8):
                    tile(n // 4, n % 4)
                with pool.Fori(2, TILES // 4) as j:
                    for r in range(4):
                        tile(j, r)
                for n in range(TILES, TILES + 4):
                    tile(n // 4, n % 4)

    return nc


_PARAMS = ["n1_g", "n1_b", "n2_g", "n2_b", "w1", "b1", "w2", "b2", "mw1", "mb1", "mw2", "mb2"]


def kernel(**inputs):
    import numpy as _np
    import concourse.bacc as _bacc
    from concourse import mybir as _mybir
    from concourse.bass_utils import run_bass_kernel_spmd as _run

    nc = _bacc.Bacc("TRN2", target_bir_lowering=False, num_devices=1)
    arrays = {}

    def given(name, a):
        a = _np.ascontiguousarray(a)
        arrays[f"in_{name}_dram"] = a
        return nc.dram_tensor(f"in_{name}_dram", a.shape, _mybir.dt.from_np(a.dtype), kind="ExternalInput").ap()

    def laid_out(layer):
        p = {n: _np.asarray(inputs[f"L{layer}_conv_{n}"]) for n in _PARAMS}

        def twice(a):
            return _np.concatenate([a, a], 0)

        def by_row(w):
            return w.reshape(2, 2, HALF, BLOCK).transpose(2, 0, 1, 3)

        b1 = p["b1"].reshape(2, 2, HALF).transpose(0, 2, 1).reshape(P, 2)
        return {
            "blocks": twice(_np.stack([by_row(p["w1"]), by_row(p["w2"])], 1)),
            "vectors": _np.stack([twice(p["n1_g"].reshape(2, HALF).T), twice(p["n1_b"].reshape(2, HALF).T), b1], 1),
            "b2": p["b2"].reshape(2, 2, HALF).transpose(1, 0, 2),
            "n1_b": p["n1_b"][None],
            "n1_g": p["n1_g"][None],
            "mw1": p["mw1"],
            "mw2": p["mw2"],
            "mb2": p["mb2"][None],
            "columns": _np.concatenate([p["n2_g"][:, None], p["n2_b"][:, None], p["mb1"].reshape(CHUNKS, P).T], 1),
        }

    x = given("x", inputs["x"])
    consts = given("consts", dft_constants())
    params = [{n: given(f"L{layer}_{n}", a) for n, a in laid_out(layer).items()} for layer in range(LAYERS)]
    out = nc.dram_tensor("out_0_dram", (IMAGES, H, W, C), _mybir.dt.float32, kind="ExternalOutput").ap()
    afno(nc, x, consts, params, out)
    r = _run(nc, [arrays], core_ids=[0])
    return r.results[0]["out_0_dram"]
```

```python
from contextlib import ExitStack

import numpy as np

import concourse.bass as bass
from concourse import mybir

F32 = mybir.dt.float32
F32R = mybir.dt.float32r
I32 = mybir.dt.int32
ALU = mybir.AluOpType
ACT = mybir.ActivationFunctionType

P = 128
IMAGES, LAYERS = 2, 2
H = W = C = 128
HALF = C // 2
BLOCK = 16
BLOCKS = HALF // BLOCK
LATENT = 4 * C
CHUNKS = LATENT // P
KWS = W // 2
ROWS = 4
TILES = H // ROWS
TOK = ROWS * W
GROUP = 4
CGROUPS = C // GROUP
BATCHES = KWS // GROUP
UNITS = 2 * BATCHES + 2
LN_EPS = 1e-5
LAM = 0.01
DC = float(np.sqrt(H * W))
MAGIC = float(0x5F3759DF - 2 ** 22 - 2 ** 30)
STEPS = [(layer, image) for layer in range(LAYERS) for image in range(IMAGES)]
LAG = 2
PRO_ACT = (7, 6, 6, 3)
CONSTS = 7 * P + 2 * BLOCKS
PAIRS = TILES // 2
EVEN = KWS + 1
PB = 8
R_DVE = 8
R_POOL0 = TILES - R_DVE
LAST = H // 2
Z_DVE0 = TILES - sum(PRO_ACT)
SPEC_IN = 16 * 4
RAW_IN = MLP_IN = 16 * 2
Y_CREDIT = 2


def row_of():
    h = np.arange(P)
    h[:HALF], h[HALF] = np.arange(1, HALF + 1), 0
    return h


def dft_constants():
    n = np.arange(P, dtype=np.float64)
    h = row_of().astype(np.float64)
    turn = 2 * np.pi / P
    scale = 1 / np.sqrt(P)
    k = np.arange(EVEN, dtype=np.float64)
    cos = np.cos(turn * np.outer(n, k)) * scale
    sin = np.sin(turn * np.outer(n, k)) * scale
    fw = np.stack([cos[:, :KWS], -sin[:, :KWS]], 2)
    fw[:, 0, 1] = cos[:, KWS]
    fh = np.concatenate([np.cos(turn * np.outer(h, k)), np.sin(turn * np.outer(h, k[1:-1]))], 1) * scale
    k_of = np.concatenate([k, -k[1:-1]])
    ih = np.concatenate([np.cos(turn * np.outer(k_of, h[:HALF + 1])),
                         np.sin(turn * np.outer(k_of, -h[HALF + 1:]))], 1) * scale
    de = 2 * np.stack([cos, -sin], 2)[:, :KWS]
    do = 2 * np.stack([-sin, -cos], 2)[:, :KWS]
    for d in (de, do):
        d[:, 0, 0], d[:, 0, 1] = cos[:, 0], cos[:, KWS]
    reverse = (k_of[:, None] % P == -k_of[None] % P).astype(np.float64)
    block = (np.arange(P) % HALF) // BLOCK
    mask = (block[:, None] == np.arange(BLOCKS)[None]).astype(np.float64)
    parts = [fw.reshape(P, P), fh, ih, de.reshape(P, P).T, do.reshape(P, P).T, np.eye(P), reverse]
    return np.concatenate([*parts, mask, -mask], 1).astype(np.float32)


class Chain:

    def __init__(self, eng, sem):
        self.eng, self.sem, self.base, self.trip, self.n = eng, sem, 0, None, 0

    def add(self, ins):
        ins.then_inc(self.sem, 1)
        self.n += 1

    def settle(self):
        at = self.base + self.n
        self.eng.wait_ge(self.sem, at if self.trip is None else self.trip * self.per + at)

    def enter(self, trip, per, first):
        self.base, self.n, self.trip, self.per = self.base + self.n - first * per, 0, trip, per

    def leave(self, end):
        assert self.n == self.per, self.n
        self.base, self.n, self.trip = self.base + end * self.per, 0, None


def afno(nc, x, consts, params, out):
    ctx = ExitStack()
    with ctx:
        top = [(nc.sbuf_base + 63) // 64 * 64]

        def at(name, shape, offset, dtype=F32):
            return nc.alloc_sbuf_tensor_at(name, shape, dtype, offset=offset)

        def size(shape):
            return int(np.prod(shape[1:])) * 4

        def sb(name, shape, dtype=F32):
            offset = top[0]
            top[0] = (offset + size(shape) + 31) // 32 * 32
            return at(name, shape, offset, dtype)

        def sem(name):
            return ctx.enter_context(nc.semaphore(name))

        resid = sb("resid", [P, H, C])
        zbuf_at = top[0]
        zbuf = sb("zbuf", [P, H, C])
        spec_at = top[0]
        spec = sb("spec", [P, KWS, 2, HALF, 2])
        spec_end = top[0]
        cst = sb("cst", [P, CONSTS])
        FW, FH, IH, DE, DO, IDENT, REVERSE = (cst[:, i * P:(i + 1) * P] for i in range(7))
        mask = cst[:, 7 * P:].rearrange("p (s b) -> p s b", s=2)
        w1s = sb("w1s", [P, 2, 2, 2, HALF])
        w2s = sb("w2s", [P, 2, 2, HALF])
        wraw = sb("wraw", [P, 2, 2, 2, BLOCK])
        vectors = sb("vectors", [P, 4, 2])
        gain64, beta64, b1v, dcbias = (vectors[:, i, :] for i in range(4))
        b2rep = sb("b2rep", [P, 2, 2, HALF])
        betarow = sb("betarow", [P, C])
        gain1 = sb("gain1", [P, C])
        columns = sb("columns", [P, 2 + CHUNKS])
        gain2, beta2, mb1 = columns[:, 0:1], columns[:, 1:2], columns[:, 2:]
        mb1f = sb("mb1f", [P, CHUNKS])
        stats = sb("stats", [P, 2, 4 * ROWS, 3])
        rstd = sb("rstd", [P, 2, 4 * ROWS])
        var = sb("var", [P, 4 * ROWS])
        shift = sb("shift", [P, 2, 2 * ROWS])
        nt0 = sb("nt0", [P, 4 * ROWS])
        gz0 = sb("gz0", [P, ROWS, C])
        xout_at = top[0]
        xout = sb("xout", [P, 2, ROWS, C])
        assert top[0] <= nc.sbuf_usable_end, (top[0], nc.sbuf_usable_end)

        mw1raw = at("mw1raw", [P, LATENT], xout_at + size([P, ROWS, C]))
        o = zbuf_at
        gsb = at("gsb", [P, 2, P, GROUP], o); o += size(gsb.shape)
        usb = at("usb", [P, 2, P, GROUP], o); o += size(usb.shape)
        osb = at("osb", [P, 2, P, GROUP], o); o += size(osb.shape)
        vsb = at("vsb", [P, 2, GROUP, 2, HALF], o); o += size(vsb.shape)
        csb = at("csb", [P, 2, GROUP, 2, HALF], o); o += size(csb.shape)
        nyq = at("nyq", [P, 2, P], o); o += size(nyq.shape)
        yedge = at("yedge", [P, 2, 2, HALF, 2], o); o += size(yedge.shape)
        tedge = at("tedge", [P, 2, 2, C], o); o += size(tedge.shape)
        assert o <= spec_at
        o = spec_at
        xnext = at("xnext", [P, 4, ROWS, C], o); o += size(xnext.shape)
        gz = at("gz", [P, 2, ROWS, C], o); o += size(gz.shape)
        hn = at("hn", [P, 2, ROWS, C], o); o += size(hn.shape)
        hth = at("hth", [P, 2, TOK], o, F32R); o += size(hth.shape)
        htl = at("htl", [P, 2, TOK], o, F32R); o += size(htl.shape)
        gel = at("gel", [P, 2, CHUNKS, TOK], o); o += size(gel.shape)
        mw1h = at("mw1h", [P, LATENT], o, F32R); o += size(mw1h.shape)
        mw1l = at("mw1l", [P, LATENT], o, F32R); o += size(mw1l.shape)
        mw2 = at("mw2", [P, CHUNKS, C], o); o += size(mw2.shape)
        mb2rep = at("mb2rep", [P, C], o); o += size(mb2rep.shape)
        assert o <= spec_end
        pst = at("pst", [P, TILES * ROWS, 3], o); o += size(pst.shape)
        prs = at("prs", [P, TILES * ROWS], o); o += size(prs.shape)
        pnm = at("pnm", [P, TILES * ROWS], o); o += size(pnm.shape)
        pva = at("pva", [P, PB * ROWS], o); o += size(pva.shape)
        pn0 = at("pn0", [P, PB * ROWS], o); o += size(pn0.shape)
        assert o <= spec_end

        ps = ctx.enter_context(nc.psum_tensor("ps", [P, 8, 512], F32))
        between = nc.dram_tensor("between", [IMAGES, H, W, C], F32).ap()

        cst_in, mask_in = sem("cst_in"), sem("mask_in")
        x_in = [sem(f"x_in{b}") for b in range(TILES // PB)]
        spec_in, gain_in, raw_in, mlp_in = sem("spec_in"), sem("gain_in"), sem("raw_in"), sem("mlp_in")
        spec_built, dc_mm, spec_done = sem("spec_built"), sem("dc_mm"), sem("spec_done")
        st_pro, z_dve, z_act, gz_done, r_done, r_dve = (
            sem(n) for n in ("st_pro", "z_dve", "z_act", "gz_done", "r_done", "r_dve"))
        s1_mm, a_act, a_dve = (sem(n) for n in ("s1_mm", "a_act", "a_dve"))
        s2_mm, m1_mm, m2_mm = sem("s2_mm"), sem("m1_mm"), sem("m2_mm")
        g_out, e_out, u_out, o_out, v_out, y_done = (
            sem(n) for n in ("g_out", "e_out", "u_out", "o_out", "v_out", "y_done"))
        t_edge, x_mm = sem("t_edge"), sem("x_mm")
        ih_mm, v_act, v_dve = sem("ih_mm"), sem("v_act"), sem("v_dve")
        mlp_w, mlp_b_mm, mlp_b = sem("mlp_w"), sem("mlp_b_mm"), sem("mlp_b")
        iw_mm, h2_done, rs_done = sem("iw_mm"), sem("h2_done"), sem("rs_done")
        hn_done, t_mm, hi_out, lo_out = sem("hn_done"), sem("t_mm"), sem("hi_out"), sem("lo_out")
        f1_mm, gelu_out, f2_mm, y_out, x_out, mb2_done = (
            sem("f1_mm"), sem("gelu_out"), sem("f2_mm"), sem("y_out"), sem("x_out"), sem("mb2_done"))
        xn_in = [sem(f"xn_in{i}") for i in range(4)]
        x_st = [sem(f"x_st{i}") for i in range(2)]
        row0_in, row0_st = sem("row0_in"), sem("row0_st")
        dve_own = sem("dve_own")

        source = [x[0], x[1], between[0], between[1]]
        target = [between[0], between[1], out[0], out[1]]

        def tile_of(j, r):
            t = 2 * j + r // 2
            return t * -1 + (TILES - 1) if r % 2 else t

        def rows(dram, h0, n):
            return dram[bass.ds(h0, n), :, :].rearrange("h w c -> w h c")

        def transfers(sp, dram, tile, j, r, done, row0, store):
            last = isinstance(j, int) and 4 * j + r == TILES - 1
            h0 = tile_of(j, r) * ROWS + (1 if r % 2 == 0 or last else 0)
            whole = [(rows(dram, h0, ROWS - last), tile[:, 1:] if last else tile, done)]
            if last:
                whole.append((rows(dram, 0, 1), tile[:, 0:1], row0))
            for far, near, signal in whole:
                sp.dma_start(far if store else near, near if store else far).then_inc(signal, 16)

        block = ctx.enter_context(nc.Block())

        def inverse_std(dve, chain, m2, v, y, t):
            chain.add(dve.tensor_scalar(v, m2, -0.5 / C, -0.5 * LN_EPS, ALU.mult, ALU.add))
            chain.settle()
            chain.add(dve.tensor_scalar(y.bitcast(I32), v.bitcast(I32), -0.5, MAGIC, ALU.mult, ALU.add))
            for _ in range(3):
                chain.settle()
                chain.add(dve.tensor_tensor(t, y, y, ALU.mult))
                chain.settle()
                chain.add(dve.tensor_tensor(t, t, v, ALU.mult))
                chain.settle()
                chain.add(dve.scalar_tensor_tensor(y, t, 1.5, y, ALU.add, ALU.mult))
            chain.settle()

        def spectrum_of(n):
            return n if isinstance(n, int) and n < 2 else n - 2

        def place(c):
            return c % HALF, c // HALF

        def evict_a(copy, q, cg, r):
            dst = spec[:, :, :, bass.ds(GROUP * cg, GROUP), q].rearrange("p k r c -> p (k r) c")
            return copy(dst, ps[:, 2 + r].rearrange("p (i k) -> p k i", i=GROUP))

        def evict_v(copy, cg, r):
            return copy(zbuf[:, :, bass.ds(GROUP * cg, GROUP)], ps[:, r].rearrange("p (i h) -> p h i", i=GROUP))

        @block.sync
        def _(sp):
            def load_spectral(layer):
                p = params[layer]
                sp.dma_start(wraw[:, :, :, :, :], p["blocks"]).then_inc(spec_in, 16)
                sp.dma_start(vectors[:, 0:3, :], p["vectors"]).then_inc(spec_in, 16)
                b2 = p["b2"].unsqueeze(0).to_broadcast([P, 2, 2, HALF])
                sp.dma_start(b2rep[:, :, :, :], b2).then_inc(spec_in, 16)
                sp.dma_start(betarow[0:1, :], p["n1_b"]).then_inc(spec_in, 16)

            def load_gain(layer):
                sp.dma_start(gain1[:, :], params[layer]["n1_g"].to_broadcast([P, C])).then_inc(gain_in, 16)

            def load_raw(layer):
                sp.dma_start(mw1raw[:, :], params[layer]["mw1"]).then_inc(raw_in, 16)
                sp.dma_start(columns[:, :], params[layer]["columns"]).then_inc(raw_in, 16)

            def load_mlp(layer):
                p = params[layer]
                sp.dma_start(mw2[:, :, :], p["mw2"].rearrange("(m k) c -> k m c", m=CHUNKS)).then_inc(mlp_in, 16)
                sp.dma_start(mb2rep[:, :], p["mb2"].to_broadcast([P, C])).then_inc(mlp_in, 16)

            n = PB * ROWS
            load_spectral(0)
            sp.dma_start(resid[:, 0:n, :], rows(source[0], 1, n)).then_inc(x_in[0], 16)
            load_gain(0)
            sp.dma_start(resid[:, n:2 * n, :], rows(source[0], n + 1, n)).then_inc(x_in[1], 16)
            sp.dma_start(resid[:, HALF, :], source[0][0]).then_inc(row0_in, 16)
            sp.dma_start(resid[:, HALF + 1:3 * n, :], rows(source[0], HALF + 1, n - 1)).then_inc(x_in[2], 16)
            sp.dma_start(resid[:, 3 * n:, :], rows(source[0], 3 * n, n)).then_inc(x_in[3], 16)

            for s, (layer, _) in enumerate(STEPS):
                last = s == len(STEPS) - 1
                sp.wait_ge(r_done, R_POOL0 + TILES * s)
                if s:
                    for i in range(2):
                        sp.wait_ge(x_st[i], 16 * (TILES // 2) * s)
                    sp.wait_ge(row0_st, 16 * s)
                load_raw(layer)
                sp.wait_ge(ih_mm, CGROUPS * (s + 1))
                load_mlp(layer)
                if not last and STEPS[s + 1][0] != layer:
                    load_gain(layer + 1)
                    load_spectral(layer + 1)

                def load(j, r):
                    sp.wait_ge(r_done, R_POOL0 + TILES * s + 4 * j + r - 3)
                    transfers(sp, source[s + 1], xnext[:, r], j, r, xn_in[r], row0_in, False)

                def store(j, r):
                    sp.wait_ge(x_out, TILES * s + 4 * j + r + 1)
                    transfers(sp, target[s], xout[:, r % 2], j, r, x_st[r % 2], row0_st, True)

                if not last:
                    for r in range(4):
                        load(0, r)
                    with sp.Fori(1, TILES // 4 - 1) as j:
                        for r in range(4):
                            store(j - 1, r)
                            load(j, r)
                    for r in range(4):
                        store(TILES // 4 - 2, r)
                        load(TILES // 4 - 1, r)
                else:
                    with sp.Fori(0, TILES // 4 - 1) as j:
                        for r in range(4):
                            store(j, r)
                for r in range(4):
                    store(TILES // 4 - 1, r)
            for i in range(2):
                sp.wait_ge(x_st[i], 16 * (TILES // 2) * len(STEPS))
            sp.wait_ge(row0_st, 16 * len(STEPS))

        @block.tensor
        def _(pe):
            def dc_bias(n):
                pe.wait_ge(spec_built, n + 1)
                if n:
                    pe.wait_ge(h2_done, TILES * IMAGES * n)
                for q in range(2):
                    mm = pe.matmul(ps[:, 7, q:q + 1], w1s[0:HALF, 0, q].rearrange("p r c -> p (r c)"),
                                   beta64[0:HALF, q:q + 1], start=(q == 0), stop=True, skip_group_check=True)
                mm.then_inc(dc_mm, 1)

            def dft_w(s):
                pe.wait_ge(z_dve, Z_DVE0 + TILES * s)
                pe.wait_ge(z_act, sum(PRO_ACT))
                for cg in range(CGROUPS):
                    if cg >= 4:
                        pe.wait_ge(a_dve if cg % 2 else a_act, CGROUPS // 2 * s + (cg - 4) // 2 + 1)
                    for i in range(GROUP):
                        mm = pe.matmul(ps[:, 2 + cg % 4, P * i:P * i + P], zbuf[:, :, GROUP * cg + i], FW,
                                       start=True, stop=True)
                    mm.then_inc(s1_mm, 1)

            def dft_h(s, n):
                g, q = spectrum_of(n), n % 2
                b = g // 2
                if g >= 2:
                    pe.wait_ge(g_out, 2 * BATCHES * s + g - 1)
                for i in range(GROUP):
                    mm = pe.matmul(ps[:, q, P * i:P * i + P],
                                   spec[:, GROUP * b + i, :, :, q].rearrange("p r c -> p (r c)"), FH,
                                   start=True, stop=True)
                mm.then_inc(s2_mm, 1)

            def mix1(s, n):
                g, q = spectrum_of(n), n % 2
                alone = n in (2, 3)
                if not alone:
                    pe.wait_ge(g_out, 2 * BATCHES * s + g + 1)
                if n >= 2:
                    pe.wait_ge(u_out, UNITS * s + n - 1)

                def both(dst, src, w_even, w_odd, start):
                    pe.matmul(dst[:, 0:EVEN], w_even, src[:, 0:EVEN], start=start, stop=True, skip_group_check=True)
                    return pe.matmul(dst[:, EVEN:], w_odd, src[:, EVEN:], start=False, stop=True,
                                     skip_group_check=True)

                even, odd = (w1s[:, i, q].rearrange("p r c -> p (r c)") for i in range(2))
                if alone:
                    dst = ps[:, 2 + q, 0:P].rearrange("p (k j) -> p k j", j=1)
                    mm = both(dst, nyq[HALF:P, q].rearrange("p (k j) -> p k j", j=1), odd[HALF:P], even[HALF:P], True)
                else:
                    dst = ps[:, 2 + q].rearrange("p (k j) -> p k j", j=GROUP)
                    src = gsb[:, q]
                    if g >= 2:
                        mm = both(dst, src, even, odd, True)
                    else:
                        both(dst[:, :, 1:], src[:, :, 1:], even, odd, True)
                        both(dst[:, :, 0:1], src[0:HALF, :, 0:1], even[0:HALF], odd[0:HALF], False)
                        mm = pe.matmul(ps[:, 2 + q, 0:1], IDENT, dcbias[:, q:q + 1], start=False, stop=True,
                                       skip_group_check=True)
                mm.then_inc(m1_mm, 1)

            def mix2(s, n):
                q, kws = n % 2, 1 if n in (2, 3) else GROUP
                pe.wait_ge(o_out, UNITS * s + n + 1)
                if n >= 2:
                    pe.wait_ge(v_out, UNITS * s + n - 1)
                src = osb[:, q].rearrange("p k j -> p (k j)")
                for i in range(kws):
                    mm = pe.matmul(ps[:, 4 + q, P * i:P * i + P], src[:, i:i + (P - 1) * kws + 1:kws],
                                   w2s[:, q].rearrange("p r c -> p (r c)"), start=True, stop=True)
                mm.then_inc(m2_mm, 1)

            def filter_(s):
                for a in (a_act, a_dve):
                    pe.wait_ge(a, CGROUPS // 2 * s + CGROUPS // 4)
                pe.wait_ge(y_out, Y_CREDIT + TILES * s)
                dft_h(s, 0)
                for a in (a_act, a_dve):
                    pe.wait_ge(a, CGROUPS // 2 * (s + 1))
                dft_h(s, 1)
                pe.wait_ge(spec_done, 1 + s // IMAGES)
                mix1(s, 0)
                for n in range(UNITS):
                    if 4 <= n + 2 < UNITS:
                        dft_h(s, n + 2)
                    if n + 1 < UNITS:
                        mix1(s, n + 1)
                    mix2(s, n)
                    if n == 5:
                        edges(s)

            def edges(s):
                pe.wait_ge(t_edge, s + 1)
                for i, m in enumerate((REVERSE, IDENT)):
                    mm = pe.matmul(ps[:, 6, 0:2 * C], m, tedge[:, i].rearrange("p k c -> p (k c)"),
                                   start=(i == 0), stop=(i == 1))
                mm.then_inc(x_mm, 1)

            def idft_h(s):
                pe.wait_ge(y_done, (UNITS + 1) * (s + 1) - 1)
                for cg in range(CGROUPS):
                    if cg == CGROUPS // 2:
                        pe.wait_ge(y_done, (UNITS + 1) * (s + 1))
                    if cg >= 4:
                        pe.wait_ge(v_dve if cg % 2 else v_act, CGROUPS // 2 * s + (cg - 4) // 2 + 1)
                    for i in range(GROUP):
                        ch, q = place(GROUP * cg + i)
                        mm = pe.matmul(ps[:, cg % 4, P * i:P * i + P],
                                       spec[:, :, :, ch, q].rearrange("p k r -> p (k r)"), IH, start=True, stop=True)
                    mm.then_inc(ih_mm, 1)

            def mlp_bias(s):
                pe.wait_ge(raw_in, RAW_IN * (s + 1))
                for m in range(CHUNKS):
                    mm = pe.matmul(ps[:, 5, m:m + 1], mw1raw[:, P * m:P * m + P], beta2[:, 0:1],
                                   start=(m == 0), stop=(m == CHUNKS - 1), skip_group_check=True)
                mm.then_inc(mlp_b_mm, 1)

            def idft_w(s, p):
                pe.wait_ge(h2_done, TILES * s + 2 * p)
                even = zbuf[:, bass.ds(p * ROWS, ROWS), :]
                odd = zbuf[:, bass.ds(p * -ROWS + (H - ROWS), ROWS), :]
                pe.matmul(ps[:, 6], DE, even, start=True, stop=True)
                if isinstance(p, int) and p == PAIRS - 1:
                    pe.matmul(ps[:, 7, C:], DO, odd[:, 1:], start=True, stop=True, skip_group_check=True)
                    mm = pe.matmul(ps[:, 7, 0:C], DE, odd[:, 0], start=False, stop=True, skip_group_check=True)
                else:
                    mm = pe.matmul(ps[:, 7], DO, odd, start=True, stop=True)
                mm.then_inc(iw_mm, 1)

            def turn(s, n, r):
                pe.wait_ge(hn_done, TILES * s + n + 1)
                if not (isinstance(n, int) and n < 2):
                    pe.wait_ge(lo_out, TILES * s + n - 1)
                for i in range(ROWS):
                    mm = pe.transpose(ps[:, 4 + r % 2, P * i:P * i + P], hn[:, r % 2, i, :], IDENT)
                mm.then_inc(t_mm, 1)

            def fc1(s, n, r, m):
                if m == 0:
                    pe.wait_ge(lo_out, TILES * s + n + 1)
                if not (isinstance(n, int) and n == 0 and m < 2):
                    pe.wait_ge(gelu_out, CHUNKS * TILES * s + CHUNKS * n + m - 1)
                h, l = mw1h[:, P * m:P * m + P], mw1l[:, P * m:P * m + P]
                bank = ps[:, 2 + m % 2]
                pe.matmul(bank, h, hth[:, r % 2, :], start=True, stop=False)
                pe.matmul(bank, h, htl[:, r % 2, :], start=False, stop=False)
                pe.matmul(bank, l, hth[:, r % 2, :], start=False, stop=True).then_inc(f1_mm, 1)

            def fc2(s, n, r, m):
                pe.wait_ge(gelu_out, CHUNKS * TILES * s + CHUNKS * n + m + 1)
                if m == 0:
                    pe.wait_ge(y_out, Y_CREDIT + TILES * s + n - 1)
                for i in range(ROWS):
                    mm = pe.matmul(ps[:, r % 2, P * i:P * i + P], gel[:, r % 2, m, P * i:P * i + P], mw2[:, m, :],
                                   start=(m == 0 and i == 0), stop=(m == CHUNKS - 1), skip_group_check=True)
                if m == CHUNKS - 1:
                    mm.then_inc(f2_mm, 1)

            def mlp(s):
                pe.wait_ge(h2_done, TILES * s)
                for half in range(2):
                    for v in (v_act, v_dve):
                        pe.wait_ge(v, CGROUPS // 2 * s + CGROUPS // 4 * (half + 1))
                    c = slice(HALF * half, HALF * half + HALF)
                    for bank, m, h0 in ((6, DE, 0), (7, DO, H - ROWS)):
                        dst = ps[:, bank].rearrange("p (h c) -> p h c", h=ROWS)[:, :, c]
                        mm = pe.matmul(dst, m, zbuf[:, h0:h0 + ROWS, c], start=(half == 0), stop=True,
                                       skip_group_check=True)
                mm.then_inc(iw_mm, 1)
                mlp_bias(s)
                idft_w(s, 1)
                turn(s, 0, 0)
                pe.wait_ge(mlp_w, s + 1)
                for m in range(CHUNKS):
                    fc1(s, 0, 0, m)
                    if m == 1:
                        pe.wait_ge(mlp_b, s + 1)
                        turn(s, 1, 1)
                pe.wait_ge(mlp_in, MLP_IN * (s + 1))

                def tile(j, r):
                    n = 4 * j + r
                    known = n if isinstance(j, int) else 4
                    for m in range(CHUNKS):
                        if known + 1 < TILES:
                            fc1(s, n + 1, r + 1, m)
                        fc2(s, n, r, m)
                        if m == 0 and r % 2 == 0 and known + 4 < TILES:
                            idft_w(s, 2 * j + r // 2 + 2)
                        if m == 1 and known + 2 < TILES:
                            turn(s, n + 2, r + 2)

                with pe.Fori(0, TILES // 4 - 2) as j:
                    for r in range(4):
                        tile(j, r)
                for n in range(TILES - 8, TILES):
                    tile(n // 4, n % 4)

            pe.wait_ge(cst_in, 16)
            for s in range(len(STEPS)):
                if s % IMAGES == 0:
                    dc_bias(s // IMAGES)
                dft_w(s)
                filter_(s)
                idft_h(s)
                mlp(s)

        @block.scalar
        def _(act):
            def a_out(s, q, j, r):
                act.wait_ge(s1_mm, CGROUPS * s + CGROUPS // 2 * q + 4 * j + r + 1)
                evict_a(act.copy, q, 4 * j + r, r).then_inc(a_act, 1)

            def g_copy(s, n, q, first=False):
                act.wait_ge(s2_mm, 2 * BATCHES * s + spectrum_of(n) + 1)
                if first:
                    act.copy(nyq[HALF:P, q], ps[HALF:P, q, 0:P])
                else:
                    act.wait_ge(m1_mm, UNITS * s + n - 1)
                src = ps[:, q].rearrange("p (j k) -> p k j", j=GROUP)
                act.copy(gsb[:, q], src).then_inc(g_out, 1)

            def e_copy(s, n, q, kws=GROUP):
                act.wait_ge(m1_mm, UNITS * s + n + 1)
                dst = usb[:, q].rearrange("p k j -> p (k j)")[:, 0:EVEN * kws]
                act.copy(dst, ps[:, 2 + q, 0:EVEN * kws]).then_inc(e_out, 1)

            def o_relu(s, n, q, kws=GROUP, first=False):
                act.wait_ge(u_out, UNITS * s + n + 1)
                if not first:
                    act.wait_ge(m2_mm, UNITS * s + n - 1)
                dst = osb[:, q].rearrange("p k j -> p (k j)")[:, 0:P * kws]
                src = usb[:, q].rearrange("p k j -> p (k j)")[:, 0:P * kws]
                act.activation(dst, src, ACT.Relu, bias=b1v[:, q:q + 1]).then_inc(o_out, 1)

            def v_out_(s, cg, r):
                act.wait_ge(ih_mm, CGROUPS * s + cg + 1)
                evict_v(act.copy, cg, r).then_inc(v_act, 1)

            def normal(s, j, r, part):
                n = 4 * j + r
                if part == 0:
                    act.wait_ge(rs_done, PAIRS * s + 2 * j + r // 2 + 1)
                    if not (isinstance(j, int) and n < 2):
                        act.wait_ge(t_mm, TILES * s + n - 1)
                for i in (2 * part, 2 * part + 1):
                    row = resid[:, bass.ds(ROWS * tile_of(j, r) + i, 1), :].rearrange("p h c -> p (h c)")
                    ins = act.activation(hn[:, r % 2, i, :], row, ACT.Identity,
                                         bias=shift[:, r // 2, r % 2 * ROWS + i:r % 2 * ROWS + i + 1],
                                         scale=rstd[:, r // 2, r % 2 * ROWS + i:r % 2 * ROWS + i + 1])
                if part:
                    ins.then_inc(hn_done, 1)

            def hi(s, n, r):
                act.wait_ge(t_mm, TILES * s + n + 1)
                act.copy(hth[:, r % 2, :], ps[:, 4 + r % 2]).then_inc(hi_out, 1)

            def y_copy(s, n, r):
                act.wait_ge(f2_mm, TILES * s + n + 1)
                if not (isinstance(n, int) and s == 0 and n < 2):
                    act.wait_ge(x_st[r % 2], 16 * (TILES // 2 * s) + (n - r % 2) * 8)
                if isinstance(n, int) and n == 1:
                    act.wait_ge(mlp_w, s + 1)
                    if s:
                        act.wait_ge(row0_st, 16 * s)
                act.copy(xout[:, r % 2].rearrange("p h c -> p (h c)"), ps[:, r % 2]).then_inc(y_out, 1)

            def gelu(s, n, r, m):
                act.wait_ge(f1_mm, CHUNKS * TILES * s + CHUNKS * n + m + 1)
                if m == 0 and not (isinstance(n, int) and n < 2):
                    act.wait_ge(f2_mm, TILES * s + n - 1)
                act.activation(gel[:, r % 2, m, :], ps[:, 2 + m % 2], ACT.Gelu, bias=mb1f[:, m:m + 1]).then_inc(
                    gelu_out, 1)

            act.dma_start(cst[:, CONSTS - 2 * BLOCKS:], consts[:, CONSTS - 2 * BLOCKS:]).then_inc(mask_in, 16)
            act.dma_start(cst[:, :CONSTS - 2 * BLOCKS], consts[:, :CONSTS - 2 * BLOCKS]).then_inc(cst_in, 16)
            for b in range(TILES // PB):
                act.wait_ge(st_pro, b + 1)
                for t in range(PB - PRO_ACT[b], PB):
                    for i in range(ROWS):
                        h = (PB * b + t) * ROWS + i
                        ins = act.activation(zbuf[:, h, :], resid[:, h, :], ACT.Identity,
                                             bias=pnm[:, h:h + 1], scale=prs[:, h:h + 1])
                    ins.then_inc(z_act, 1)
            for s in range(len(STEPS)):
                if s:
                    act.wait_ge(r_done, R_POOL0 + TILES * s)
                for q in range(2):
                    with act.Fori(0, CGROUPS // 8) as j:
                        for r in (0, 2):
                            a_out(s, q, j, r)
                act.wait_ge(r_done, R_POOL0 + TILES * s)
                act.wait_ge(r_dve, R_DVE)
                for q in range(2):
                    g_copy(s, q, q, first=True)
                for q in range(2):
                    e_copy(s, q, q)
                    o_relu(s, q, q, first=True)
                for q in range(2):
                    e_copy(s, 2 + q, q, kws=1)
                    o_relu(s, 2 + q, q, kws=1)
                    if q == 0:
                        g_copy(s, 4, 0)

                def batch(b, last=False):
                    n = 2 * b + 2
                    g_copy(s, n + 1, 1)
                    e_copy(s, n, 0)
                    o_relu(s, n, 0)
                    if not last:
                        g_copy(s, n + 2, 0)
                    e_copy(s, n + 1, 1)
                    o_relu(s, n + 1, 1)

                with act.Fori(1, BATCHES - 1) as b:
                    batch(b)
                batch(BATCHES - 1, last=True)
                act.wait_ge(y_done, (UNITS + 1) * (s + 1))
                with act.Fori(0, CGROUPS // 4) as j:
                    for r in (0, 2):
                        v_out_(s, 4 * j + r, r)
                for n in range(2):
                    for part in range(2):
                        normal(s, 0, n, part)
                    if n == 0:
                        hi(s, 0, 0)
                act.wait_ge(mlp_b, s + 1)
                for m in range(CHUNKS):
                    if m == 2:
                        hi(s, 1, 1)
                    gelu(s, 0, 0, m)

                def tile(j, r):
                    n = 4 * j + r
                    known = n if isinstance(j, int) else 4
                    for m in range(CHUNKS):
                        if m == 1 and known:
                            y_copy(s, n - 1, (r - 1) % 4)
                        if m == 2 and known + 2 < TILES:
                            hi(s, n + 2, (r + 2) % 4)
                        if known + 1 < TILES:
                            gelu(s, n + 1, (r + 1) % 4, m)
                        if m == 0 and known + 2 < TILES:
                            normal(s, j + (r + 2) // 4, (r + 2) % 4, 1)
                        if m == 3 and known + 3 < TILES:
                            normal(s, j + (r + 3) // 4, (r + 3) % 4, 0)

                normal(s, 0, 2, 0)
                for r in range(4):
                    tile(0, r)
                with act.Fori(1, TILES // 4 - 1) as j:
                    for r in range(4):
                        tile(j, r)
                for r in range(4):
                    tile(TILES // 4 - 1, r)

        @block.vector
        def _(dve):
            own = Chain(dve, dve_own)

            def build_spectral(n):
                dve.wait_ge(spec_in, SPEC_IN * (n + 1))
                if n:
                    dve.wait_ge(ih_mm, CGROUPS * n * IMAGES)
                re, im = slice(0, HALF), slice(HALF, P)
                jobs = [(w1s[:, 0], wraw[:, 0], [(re, 0, 0, 0), (re, 1, 1, 0), (im, 0, 1, 1), (im, 1, 0, 0)]),
                        (w1s[:, 1], wraw[:, 0], [(re, 0, 1, 0), (re, 1, 0, 1), (im, 0, 0, 0), (im, 1, 1, 0)]),
                        (w2s[:, :], wraw[:, 1], [(re, 0, 0, 0), (re, 1, 1, 0), (im, 0, 1, 1), (im, 1, 0, 0)])]
                for dst, raw, parts in jobs:
                    for part, col, j, sign in parts:
                        for q in range(2):
                            src = raw[part, j, q, :].unsqueeze(1).to_broadcast([HALF, BLOCKS, BLOCK])
                            m = mask[part, sign, :].unsqueeze(2).to_broadcast([HALF, BLOCKS, BLOCK])
                            to = dst[part, q, col, :].rearrange("p (b o) -> p b o", b=BLOCKS)
                            own.add(dve.tensor_tensor(to, src, m, ALU.mult))
                own.settle()
                dve.nop().then_inc(spec_built, 1)
                dve.wait_ge(dc_mm, n + 1)
                own.add(dve.tensor_scalar(dcbias[:, :], ps[:, 7, 0:2], DC, None, ALU.mult))
                own.add(dve.tensor_scalar(betarow[0:1, :], betarow[0:1, :], DC, None, ALU.mult))
                for q in range(2):
                    for kind in range(2):
                        t = w1s[:, kind, q].rearrange("p r c -> p (r c)")
                        own.add(dve.tensor_scalar(t, t, gain64[:, q:q + 1], None, ALU.mult))
                own.settle()
                dve.nop().then_inc(spec_done, 1)

            def bn(buf, row, to):
                for i in range(ROWS - 2, -1, -2):
                    src = buf[:, bass.ds(row + i, 2), :].rearrange("p h c -> p c h")
                    ins = dve.bn_stats(to[:, i:i + 2, :].rearrange("p h k -> p (h k)"), src)
                return ins

            dve.wait_ge(mask_in, 16)
            dve.nop().then_inc(y_out, Y_CREDIT)
            build_spectral(0)
            for b in range(TILES // PB):
                dve.wait_ge(x_in[b], 16)
                if b == TILES // PB // 2:
                    dve.wait_ge(row0_in, 16)
                h0 = PB * ROWS * b
                own_rows = slice(h0, h0 + PB * ROWS)
                for t in range(PB):
                    h = h0 + ROWS * t
                    own.add(bn(resid, h, pst[:, h:h + ROWS, :]))
                own.settle()
                inverse_std(dve, own, pst[:, own_rows, 2], pva[:, :], prs[:, own_rows], pn0[:, :])
                own.add(dve.scalar_tensor_tensor(pnm[:, own_rows], pst[:, own_rows, 1], -1.0, prs[:, own_rows],
                                                 ALU.mult, ALU.mult))
                own.settle()
                dve.nop().then_inc(st_pro, 1)
                for t in range(PB - PRO_ACT[b]):
                    for i in range(ROWS):
                        h = h0 + ROWS * t + i
                        ins = dve.tensor_scalar(zbuf[:, h, :], resid[:, h, :], pst[:, h, 1:2], prs[:, h:h + 1],
                                                ALU.subtract, ALU.mult)
                    ins.then_inc(z_dve, 1)

            def a_out(s, q, j, r):
                dve.wait_ge(s1_mm, CGROUPS * s + CGROUPS // 2 * q + 4 * j + r + 1)
                evict_a(dve.tensor_copy, q, 4 * j + r, r).then_inc(a_dve, 1)

            def residual(t):
                if t == R_POOL0:
                    dve.wait_ge(gain_in, 16)
                    dve.wait_ge(z_dve, Z_DVE0)
                    dve.wait_ge(z_act, sum(PRO_ACT))
                else:
                    dve.wait_ge(r_dve, t - R_POOL0)
                h = slice(ROWS * t, ROWS * t + ROWS)
                g = gain1[:, :].unsqueeze(1).to_broadcast([P, ROWS, C])
                own.add(dve.tensor_tensor(gz0[:, :, :], zbuf[:, h, :], g, ALU.mult))
                own.settle()
                dve.tensor_tensor(resid[:, h, :], resid[:, h, :], gz0[:, :, :], ALU.add).then_inc(r_dve, 1)

            def combine(s, n, q, kws=GROUP):
                dve.wait_ge(e_out, UNITS * s + n + 1)
                odd = ps[:, 2 + q, EVEN * kws:P * kws].rearrange("p (k j) -> p k j", j=kws)
                u = usb[:, q].rearrange("p k j -> p (k j)")[:, 0:P * kws].rearrange("p (k j) -> p k j", j=kws)
                ops = (ALU.add, ALU.subtract) if kws > 1 else (ALU.subtract, ALU.add)
                dve.tensor_tensor(u[:, EVEN:], u[:, 1:KWS], odd, ops[1])
                ins = dve.tensor_tensor(u[:, 1:KWS], u[:, 1:KWS], odd, ops[0])
                ins.then_inc(u_out, 1)

            def shrink(s, n, b, q, kws=GROUP):
                dve.wait_ge(m2_mm, UNITS * s + n + 1)
                bias = b2rep[:, q].rearrange("p r c -> p (r c)").unsqueeze(1).to_broadcast([P, kws, P])
                v = vsb[:, q].rearrange("p j r c -> p j (r c)")[:, 0:kws]
                cl = csb[:, q].rearrange("p j r c -> p j (r c)")[:, 0:kws]
                src = ps[:, 4 + q, 0:P * kws].rearrange("p (j k) -> p j k", j=kws)
                dve.tensor_tensor(v, src, bias, ALU.add).then_inc(v_out, 1)
                dve.wait_ge(v_out, UNITS * s + n + 1)
                own.add(dve.tensor_scalar(cl, v, -LAM, LAM, ALU.max, ALU.min))
                own.settle()
                v, cl = vsb[:, q], csb[:, q]
                if kws == 1 or isinstance(b, int) and b == 0:
                    edge = yedge[:, 0 if kws > 1 else 1, :, :, q]
                    ins = dve.tensor_tensor(edge, v[:, 0], cl[:, 0], ALU.subtract)
                    if kws == 1:
                        ins.then_inc(y_done, 1)
                        return
                    own.add(ins)
                    dst, v, cl = spec[:, 1:GROUP, :, :, q], v[:, 1:], cl[:, 1:]
                else:
                    dst = spec[:, bass.ds(GROUP * b, GROUP), :, :, q]
                dve.tensor_tensor(dst, v, cl, ALU.subtract).then_inc(y_done, 1)

            def edges(s):
                dve.wait_ge(y_done, (UNITS + 1) * s + 4)
                own.settle()
                shift = yedge[0:1, 0, 0].rearrange("p c q -> p q c")
                own.add(dve.tensor_tensor(shift, shift, betarow[0:1, :].rearrange("p (q c) -> p q c", q=2), ALU.add))
                own.settle()
                for i, op in enumerate((ALU.add, ALU.subtract)):
                    ins = dve.tensor_tensor(tedge[:, i], yedge[:, :, 0].rearrange("p k c q -> p k (c q)"),
                                            yedge[:, :, 1].rearrange("p k c q -> p k (c q)"), op)
                ins.then_inc(t_edge, 1)

            def edges_out(s):
                dve.wait_ge(x_mm, s + 1)
                dve.tensor_scalar(spec[:, 0].rearrange("p r c q -> p (r c q)"), ps[:, 6, 0:2 * C], 0.5, None,
                                  ALU.mult).then_inc(y_done, 1)

            def v_out_(s, cg, r):
                dve.wait_ge(ih_mm, CGROUPS * s + cg + 1)
                evict_v(dve.tensor_copy, cg, r).then_inc(v_dve, 1)

            def split_weights(s):
                dve.wait_ge(raw_in, RAW_IN * (s + 1))
                own.add(dve.tensor_scalar(mw1h[:, :], mw1raw[:, :], gain2[:, 0:1], None, ALU.mult))
                own.settle()
                dve.scalar_tensor_tensor(mw1l[:, :], mw1raw[:, :], gain2[:, 0:1], mw1h[:, :].bitcast(F32),
                                         ALU.mult, ALU.subtract).then_inc(mlp_w, 1)

            def shift_bias(s):
                dve.wait_ge(mlp_b_mm, s + 1)
                dve.tensor_tensor(mb1f[:, :], ps[:, 5, 0:CHUNKS], mb1[:, :], ALU.add).then_inc(mlp_b, 1)

            def rows_of(buf, j, r, n=ROWS, i=0):
                return buf[:, bass.ds(ROWS * tile_of(j, r) + i, n), :].rearrange("p h c -> p (h c)")

            def h2(s, i, h):
                dve.wait_ge(iw_mm, PAIRS * s + 2 * i + h + 1)
                last = isinstance(i, int) and 2 * i + h == PAIRS - 1
                top, low = (resid[:, bass.ds(ROWS * tile_of(i, 2 * h + e), ROWS), :] for e in range(2))
                even = ps[:, 6].rearrange("p (h c) -> p h c", h=ROWS)
                odd = ps[:, 7].rearrange("p (h c) -> p h c", h=ROWS)
                own.add(dve.tensor_tensor(top, even, top, ALU.add))
                if last:
                    dve.tensor_tensor(low[:, 0:1], odd[:, 0:1], low[:, 0:1], ALU.add)
                    own.add(dve.tensor_tensor(low[:, 1:], even[:, 2::-1], low[:, 1:], ALU.add))
                    own.settle()
                    dve.tensor_tensor(top[:, 0:3], odd[:, :0:-1], top[:, 0:3], ALU.add)
                    ins = dve.tensor_tensor(low[:, 1:], low[:, 1:], odd[:, 1:], ALU.subtract)
                else:
                    own.add(dve.tensor_tensor(low, even[:, ::-1], low, ALU.add))
                    own.settle()
                    dve.tensor_tensor(top, odd[:, ::-1], top, ALU.add)
                    ins = dve.tensor_tensor(low, low, odd, ALU.subtract)
                ins.then_inc(h2_done, 2)

            def lower(s, n, r):
                dve.wait_ge(hi_out, TILES * s + n + 1)
                dve.tensor_tensor(htl[:, r % 2, :], ps[:, 4 + r % 2], hth[:, r % 2, :].bitcast(F32),
                                  ALU.subtract).then_inc(lo_out, 1)

            def z_new(i, h, e):
                for k in range(ROWS):
                    row = 2 * ROWS + e * ROWS + k
                    ins = dve.tensor_scalar(rows_of(zbuf, i, 2 * h + e, 1, k), xnext[:, 2 * h + e, k, :],
                                            stats[:, h, row, 1:2], rstd[:, h, row:row + 1],
                                            ALU.subtract, ALU.mult)
                ins.then_inc(z_dve, 1)

            def last_tile(s, last):
                dve.wait_ge(f2_mm, TILES * (s + 1))
                dve.wait_ge(mb2_done, TILES * (s + 1))
                dve.wait_ge(x_st[1], 16 * (TILES // 2 * (s + 1) - 1))
                dve.wait_ge(x_out, TILES * (s + 1) - 1)
                t = resid[:, LAST:LAST + ROWS, :].rearrange("p h c -> p (h c)")
                dve.tensor_tensor(xout[:, 1].rearrange("p h c -> p (h c)"), ps[:, 1], t, ALU.add).then_inc(x_out, 1)
                dve.wait_ge(x_out, TILES * (s + 1))
                dve.nop().then_inc(y_out, 1)
                if not last:
                    dve.wait_ge(gz_done, R_POOL0 + TILES * (s + 1))
                    dve.tensor_tensor(resid[:, LAST:LAST + ROWS, :], xnext[:, 3], gz[:, 1], ALU.add).then_inc(
                        r_done, 1)

            for s in range(len(STEPS)):
                last = s == len(STEPS) - 1
                if s:
                    dve.wait_ge(r_done, R_POOL0 + TILES * s)
                for q in range(2):
                    if s == 0:
                        for j in range(CGROUPS // 8):
                            for r in (1, 3):
                                a_out(s, q, j, r)
                            residual(R_POOL0 + q * CGROUPS // 8 + j)
                    else:
                        with dve.Fori(0, CGROUPS // 8) as j:
                            for r in (1, 3):
                                a_out(s, q, j, r)
                combine(s, 0, 0)
                combine(s, 1, 1)
                shrink(s, 0, 0, 0)
                combine(s, 2, 0, kws=1)
                shrink(s, 1, 0, 1)
                combine(s, 3, 1, kws=1)
                shrink(s, 2, BATCHES, 0, kws=1)
                combine(s, 4, 0)
                shrink(s, 3, BATCHES, 1, kws=1)
                edges(s)

                def batch(b, last=False):
                    for q in range(2):
                        if not (last and q):
                            combine(s, 2 * b + 3 + q, 1 - q)
                        shrink(s, 2 * b + 2 + q, b, q)

                batch(1)
                edges_out(s)
                with dve.Fori(2, BATCHES - 1) as b:
                    own.enter(b, 2, 2)
                    batch(b)
                own.leave(BATCHES - 1)
                batch(BATCHES - 1, last=True)
                dve.wait_ge(y_done, (UNITS + 1) * (s + 1))
                with dve.Fori(0, CGROUPS // 4) as j:
                    for r in (1, 3):
                        v_out_(s, 4 * j + r, r)

                def pair(i, h):
                    q = 2 * i + h
                    known = q if isinstance(i, int) else 4
                    main = known < PAIRS
                    nxt = not last and known >= LAG
                    if main:
                        if known >= 2:
                            dve.wait_ge(hn_done, TILES * s + 2 * q - 2)
                        h2(s, i, h)
                    if 1 <= known <= PAIRS:
                        lower(s, 2 * q - 2, (2 * h - 2) % 4)
                    if main:
                        dve.wait_ge(h2_done, TILES * s + 2 * q + 2)
                        for e in range(2):
                            ins = bn(resid, tile_of(i, 2 * h + e) * ROWS, stats[:, h, e * ROWS:(e + 1) * ROWS, :])
                    if nxt:
                        for e in range(2):
                            dve.wait_ge(xn_in[2 * h + e], 16 * (TILES // 4 * s + i))
                            if isinstance(i, int) and 2 * (q - LAG) + e == TILES - 1:
                                dve.wait_ge(row0_in, 16 * (s + 2))
                            rows_ = slice((2 + e) * ROWS, (3 + e) * ROWS)
                            ins = bn(xnext[:, 2 * h + e], 0, stats[:, h, rows_, :])
                    if main or nxt:
                        own.add(ins)
                        own.settle()
                        a, b = 0 if main else 2 * ROWS, 4 * ROWS if nxt else 2 * ROWS
                        inverse_std(dve, own, stats[:, h, a:b, 2], var[:, a:b], rstd[:, h, a:b], nt0[:, a:b])
                    if main:
                        dve.scalar_tensor_tensor(shift[:, h], stats[:, h, 0:2 * ROWS, 1], -1.0, rstd[:, h, 0:2 * ROWS],
                                                 ALU.mult, ALU.mult).then_inc(rs_done, 1)
                    if nxt:
                        z_new(i - 1, h, 0)
                        z_new(i - 1, h, 1)
                    if 1 <= known <= PAIRS:
                        lower(s, 2 * q - 1, (2 * h - 1) % 4)

                pair(0, 0)
                split_weights(s)
                shift_bias(s)
                pair(0, 1)
                with dve.Fori(1, PAIRS // 2 - 1) as i:
                    own.enter(i, 2 * 14, 1)
                    for h in range(2):
                        pair(i, h)
                own.leave(PAIRS // 2 - 1)
                for q in range(PAIRS - 2, PAIRS + LAG):
                    pair(q // 2, q % 2)
                if s + 1 < len(STEPS) and STEPS[s + 1][0] != STEPS[s][0]:
                    build_spectral(STEPS[s + 1][0])
                last_tile(s, last)

        @block.gpsimd
        def _(pool):

            def scale(h0, tmp):
                z = zbuf[:, h0, :]
                g = gain1[:, :].unsqueeze(1).to_broadcast([P, ROWS, C])
                pool.tensor_tensor(tmp, z, g, ALU.mult).then_inc(gz_done, 1)

            def residual(h0, xtile, tmp):
                pool.tensor_tensor(resid[:, h0, :], xtile, tmp, ALU.add).then_inc(r_done, 1)

            pool.wait_ge(gain_in, 16)
            done = [0, 0]
            for t in range(R_POOL0):
                who = 0 if t % PB < PB - PRO_ACT[t // PB] else 1
                done[who] += 1
                pool.wait_ge((z_dve, z_act)[who], done[who])
                if t >= 2:
                    pool.wait_ge(r_done, t - 1)
                h = slice(ROWS * t, ROWS * t + ROWS)
                scale(h, xout[:, t % 2])
                pool.wait_ge(gz_done, t + 1)
                residual(h, resid[:, h, :], xout[:, t % 2])

            for s in range(len(STEPS)):
                last = s == len(STEPS) - 1
                if not last and STEPS[s + 1][0] != STEPS[s][0]:
                    pool.wait_ge(gain_in, 16 * 2)

                pool.wait_ge(mlp_in, MLP_IN * (s + 1))

                def x_new(s, j, r):
                    n = 4 * j + r
                    pool.wait_ge(y_out, Y_CREDIT + TILES * s + n + 1)
                    pool.wait_ge(mb2_done, TILES * s + n + 1)
                    first = 2 * ROWS * j + r // 2 * ROWS
                    if r % 2:
                        first = first * -1 + (H - ROWS)
                    t = resid[:, bass.ds(first, ROWS), :].rearrange("p h c -> p (h c)")
                    y = xout[:, r % 2].rearrange("p h c -> p (h c)")
                    pool.tensor_tensor(y, y, t, ALU.add).then_inc(x_out, 1)

                def bias(s, j, r):
                    t = resid[:, bass.ds(ROWS * tile_of(j, r), ROWS), :]
                    b = mb2rep[:, :].unsqueeze(1).to_broadcast([P, ROWS, C])
                    pool.tensor_tensor(t, t, b, ALU.add).then_inc(mb2_done, 1)

                def tile(j, r):
                    n = 4 * j + r
                    known = n if isinstance(j, int) else 8
                    nxt = not last
                    main = known < TILES
                    m = n - 4
                    again = nxt and known >= 4
                    if again:
                        h0 = bass.ds(ROWS * tile_of(j - 1, r), ROWS)
                        pool.wait_ge(z_dve, Z_DVE0 + TILES * s + m + 1)
                        pool.wait_ge(r_done, R_POOL0 + TILES * s + m - 1)
                        scale(h0, gz[:, r % 2])
                    if again and known == TILES + 2:
                        pool.wait_ge(z_dve, Z_DVE0 + TILES * (s + 1))
                        pool.wait_ge(r_done, R_POOL0 + TILES * s + m)
                        scale(slice(LAST, LAST + ROWS), gz[:, 1])
                    if 4 <= known < TILES + 4:
                        x_new(s, j - 1, r)
                    if again:
                        pool.wait_ge(gz_done, R_POOL0 + TILES * s + m + 1)
                        pool.wait_ge(x_out, TILES * s + m + 1)
                    if 2 <= known <= TILES + 1:
                        pool.wait_ge(hn_done, TILES * s + n - 1)
                        bias(s, j + (r - 2) // 4, (r - 2) % 4)
                    if again:
                        residual(h0, xnext[:, r], gz[:, r % 2])

                for n in range(8):
                    tile(n // 4, n % 4)
                with pool.Fori(2, TILES // 4) as j:
                    for r in range(4):
                        tile(j, r)
                for n in range(TILES, TILES + 3):
                    tile(n // 4, n % 4)

    return nc


_PARAMS = ["n1_g", "n1_b", "n2_g", "n2_b", "w1", "b1", "w2", "b2", "mw1", "mb1", "mw2", "mb2"]


def kernel(**inputs):
    import numpy as _np
    import concourse.bacc as _bacc
    from concourse import mybir as _mybir
    from concourse.bass_utils import run_bass_kernel_spmd as _run

    nc = _bacc.Bacc("TRN2", target_bir_lowering=False, num_devices=1)
    arrays = {}

    def given(name, a):
        a = _np.ascontiguousarray(a)
        arrays[f"in_{name}_dram"] = a
        return nc.dram_tensor(f"in_{name}_dram", a.shape, _mybir.dt.from_np(a.dtype), kind="ExternalInput").ap()

    def laid_out(layer):
        p = {n: _np.asarray(inputs[f"L{layer}_conv_{n}"]) for n in _PARAMS}

        def twice(a):
            return _np.concatenate([a, a], 0)

        def by_row(w):
            return w.reshape(2, 2, HALF, BLOCK).transpose(2, 0, 1, 3)

        b1 = p["b1"].reshape(2, 2, HALF).transpose(0, 2, 1).reshape(P, 2)
        return {
            "blocks": twice(_np.stack([by_row(p["w1"]), by_row(p["w2"])], 1)),
            "vectors": _np.stack([twice(p["n1_g"].reshape(2, HALF).T), twice(p["n1_b"].reshape(2, HALF).T), b1], 1),
            "b2": p["b2"].reshape(2, 2, HALF).transpose(1, 0, 2),
            "n1_b": p["n1_b"][None],
            "n1_g": p["n1_g"][None],
            "mw1": p["mw1"],
            "mw2": p["mw2"],
            "mb2": p["mb2"][None],
            "columns": _np.concatenate([p["n2_g"][:, None], p["n2_b"][:, None], p["mb1"].reshape(CHUNKS, P).T], 1),
        }

    x = given("x", inputs["x"])
    consts = given("consts", dft_constants())
    params = [{n: given(f"L{layer}_{n}", a) for n, a in laid_out(layer).items()} for layer in range(LAYERS)]
    out = nc.dram_tensor("out_0_dram", (IMAGES, H, W, C), _mybir.dt.float32, kind="ExternalOutput").ap()
    afno(nc, x, consts, params, out)
    r = _run(nc, [arrays], core_ids=[0])
    return r.results[0]["out_0_dram"]
```
